# Optimizing a Trainium2 kernel written in Bass

```python
import numpy as np
import jax
import jax.numpy as jnp

def _softmax(x, axis=-1):
    return jax.nn.softmax(x, axis=axis)

def _gelu(x):
    return jax.nn.gelu(x, approximate=True)

def _silu(x):
    return jax.nn.silu(x)

def _sigmoid(x):
    return jax.nn.sigmoid(x)

def _layernorm(x, axis=-1, eps=1e-05):
    m = jnp.mean(x, axis=axis, keepdims=True)
    v = jnp.var(x, axis=axis, keepdims=True)
    return (x - m) / jnp.sqrt(v + eps)

def _scatter_add(tgt, idx, src, axis=0):
    return tgt.at[idx].add(src)

def _segment_sum(src, seg, n):
    return jax.ops.segment_sum(src, seg, n)
kernel_name = 'mk_seq_postln_d1_jaxref_r8_65ff3b'

def setup_inputs(seed: int=0):
    np.random.seed(seed)
    _w = jnp.asarray

    def _L0_attn_setup():
        import jax, jax.numpy as jnp
        import numpy as np
        B, S, H, HS, BLK = (4, 512, 16, 128, 64)
        D = HS // H
        key = jax.random.key(seed)
        ks = jax.random.split(key, 7)
        s = np.float32(1.0 / np.sqrt(HS))
        return {'hidden_states': jax.random.normal(ks[0], (B, S, HS), jnp.float32), 'Wq': jax.random.normal(ks[1], (HS, HS), jnp.float32) * s, 'bq': jax.random.normal(ks[2], (HS,), jnp.float32) * s, 'Wk': jax.random.normal(ks[3], (HS, HS), jnp.float32) * s, 'bk': jax.random.normal(ks[4], (HS,), jnp.float32) * s, 'Wv': jax.random.normal(ks[5], (HS, HS), jnp.float32) * s, 'bv': jax.random.normal(ks[6], (HS,), jnp.float32) * s}
    _L0_attn_in = _L0_attn_setup()

    def _L0_ffn_setup():
        import jax, jax.numpy as jnp
        import numpy as np
        B, S, H, NH, E, F = (4, 128, 128, 16, 8, 512)
        D = H // NH
        EPS = 1e-05

        def _layernorm(x, g, b):
            mu = jnp.mean(x, axis=-1, keepdims=True)
            var = jnp.var(x, axis=-1, keepdims=True)
            return (x - mu) * jax.lax.rsqrt(var + EPS) * g + b
        key = jax.random.key(seed)
        ks = jax.random.split(key, 16)
        s = 0.02
        return {'x': jax.random.normal(ks[0], (B, S, H), jnp.float32), 'ln1_g': jnp.ones((H,), jnp.float32), 'ln1_b': jnp.zeros((H,), jnp.float32), 'ln2_g': jnp.ones((H,), jnp.float32), 'ln2_b': jnp.zeros((H,), jnp.float32), 'wq': jax.random.normal(ks[1], (H, H), jnp.float32) * s, 'bq': jnp.zeros((H,), jnp.float32), 'wk': jax.random.normal(ks[2], (H, H), jnp.float32) * s, 'bk': jnp.zeros((H,), jnp.float32), 'wv': jax.random.normal(ks[3], (H, H), jnp.float32) * s, 'bv': jnp.zeros((H,), jnp.float32), 'wo': jax.random.normal(ks[4], (H, H), jnp.float32) * s, 'bo': jnp.zeros((H,), jnp.float32), 'gate_w': jax.random.normal(ks[5], (H, E), jnp.float32) * s, 'gate_b': jnp.zeros((E,), jnp.float32), 'w1': jax.random.normal(ks[6], (E, H, F), jnp.float32) * s, 'b1': jnp.zeros((E, F), jnp.float32), 'w2': jax.random.normal(ks[7], (E, F, H), jnp.float32) * s, 'b2': jnp.zeros((E, H), jnp.float32)}
    _L0_ffn_in = _L0_ffn_setup()
    _d = {'L0_attn_hidden_states': _L0_attn_in['hidden_states'], 'L0_attn_Wq': _L0_attn_in['Wq'], 'L0_attn_bq': _L0_attn_in['bq'], 'L0_attn_Wk': _L0_attn_in['Wk'], 'L0_attn_bk': _L0_attn_in['bk'], 'L0_attn_Wv': _L0_attn_in['Wv'], 'L0_attn_bv': _L0_attn_in['bv'], 'L0_ffn_ln1_g': _L0_ffn_in['ln1_g'], 'L0_ffn_ln1_b': _L0_ffn_in['ln1_b'], 'L0_ffn_ln2_g': _L0_ffn_in['ln2_g'], 'L0_ffn_ln2_b': _L0_ffn_in['ln2_b'], 'L0_ffn_wq': _L0_ffn_in['wq'], 'L0_ffn_bq': _L0_ffn_in['bq'], 'L0_ffn_wk': _L0_ffn_in['wk'], 'L0_ffn_bk': _L0_ffn_in['bk'], 'L0_ffn_wv': _L0_ffn_in['wv'], 'L0_ffn_bv': _L0_ffn_in['bv'], 'L0_ffn_wo': _L0_ffn_in['wo'], 'L0_ffn_bo': _L0_ffn_in['bo'], 'L0_ffn_gate_w': _L0_ffn_in['gate_w'], 'L0_ffn_gate_b': _L0_ffn_in['gate_b'], 'L0_ffn_w1': _L0_ffn_in['w1'], 'L0_ffn_b1': _L0_ffn_in['b1'], 'L0_ffn_w2': _L0_ffn_in['w2'], 'L0_ffn_b2': _L0_ffn_in['b2']}
    _x0 = _d['L0_attn_hidden_states']
    _d['L0_attn_hidden_states'] = jax.random.normal(jax.random.fold_in(jax.random.key(seed), 1), (2, 1024, 128), dtype=_x0.dtype)
    del _x0
    return _d

def reference(L0_attn_hidden_states, L0_attn_Wq, L0_attn_bq, L0_attn_Wk, L0_attn_bk, L0_attn_Wv, L0_attn_bv, L0_ffn_ln1_g, L0_ffn_ln1_b, L0_ffn_ln2_g, L0_ffn_ln2_b, L0_ffn_wq, L0_ffn_bq, L0_ffn_wk, L0_ffn_bk, L0_ffn_wv, L0_ffn_bv, L0_ffn_wo, L0_ffn_bo, L0_ffn_gate_w, L0_ffn_gate_b, L0_ffn_w1, L0_ffn_b1, L0_ffn_w2, L0_ffn_b2):

    def _L0_attn_ref(hidden_states, Wq, bq, Wk, bk, Wv, bv):
        import jax, jax.numpy as jnp
        import numpy as np
        B, S, H, HS, BLK = (4, 512, 16, 128, 64)
        D = HS // H
        b, m, _ = hidden_states.shape
        h, d, wm = (H, D, BLK)
        wn = wm
        nb = m // wm
        scale = np.float32(1.0 / np.sqrt(d))

        def heads(x):
            return x.reshape(b, m, h, d).transpose(0, 2, 1, 3)
        q = heads(hidden_states @ Wq.T + bq)
        k = heads(hidden_states @ Wk.T + bk)
        v = heads(hidden_states @ Wv.T + bv)
        qb = q.reshape(b, h, nb, wm, d)
        kb = k.reshape(b, h, nb, wn, d)
        vb = v.reshape(b, h, nb, wn, d)

        def attend(qx, kx, vx):
            scores = jnp.einsum('bhqd,bhkd->bhqk', qx, kx) * scale
            return jnp.einsum('bhqk,bhkd->bhqd', jax.nn.softmax(scores, axis=-1), vx)
        first_ctx = attend(qb[:, :, 0], k, v)[:, :, None]
        k2 = jnp.concatenate([kb[:, :, 0], kb[:, :, 1], kb[:, :, 2], kb[:, :, -1]], axis=2)
        v2 = jnp.concatenate([vb[:, :, 0], vb[:, :, 1], vb[:, :, 2], vb[:, :, -1]], axis=2)
        second_ctx = attend(qb[:, :, 1], k2, v2)[:, :, None]
        exp_k = jnp.concatenate([kb[:, :, 1:-3], kb[:, :, 2:-2], kb[:, :, 3:-1]], axis=3)
        exp_v = jnp.concatenate([vb[:, :, 1:-3], vb[:, :, 2:-2], vb[:, :, 3:-1]], axis=3)
        mq = qb[:, :, 2:-2]
        inner = jnp.einsum('bhlqd,bhlkd->bhlqk', mq, exp_k) * scale
        first_band = jnp.einsum('bhlqd,bhkd->bhlqk', mq, kb[:, :, 0]) * scale
        last_band = jnp.einsum('bhlqd,bhkd->bhlqk', mq, kb[:, :, -1]) * scale
        band = jnp.concatenate([first_band, inner, last_band], axis=-1)
        aw = jax.nn.softmax(band, axis=-1)
        mid_ctx = jnp.einsum('bhlqk,bhlkd->bhlqd', aw[..., wn:4 * wn], exp_v)
        mid_ctx = mid_ctx + jnp.einsum('bhlqk,bhkd->bhlqd', aw[..., :wn], vb[:, :, 0])
        mid_ctx = mid_ctx + jnp.einsum('bhlqk,bhkd->bhlqd', aw[..., -wn:], vb[:, :, -1])
        k3 = jnp.concatenate([kb[:, :, 0], kb[:, :, -3], kb[:, :, -2], kb[:, :, -1]], axis=2)
        v3 = jnp.concatenate([vb[:, :, 0], vb[:, :, -3], vb[:, :, -2], vb[:, :, -1]], axis=2)
        second_last_ctx = attend(qb[:, :, -2], k3, v3)[:, :, None]
        last_ctx = attend(qb[:, :, -1], k, v)[:, :, None]
        ctx = jnp.concatenate([first_ctx, second_ctx, mid_ctx, second_last_ctx, last_ctx], axis=2)
        return ctx.reshape(b, h, m, d).transpose(0, 2, 1, 3).reshape(b, m, h * d)

    def _L0_ffn_ref(x, ln1_g, ln1_b, ln2_g, ln2_b, wq, bq, wk, bk, wv, bv, wo, bo, gate_w, gate_b, w1, b1, w2, b2):
        import jax, jax.numpy as jnp
        import numpy as np
        B, S, H, NH, E, F = (4, 128, 128, 16, 8, 512)
        D = H // NH
        EPS = 1e-05

        def _layernorm(x, g, b):
            mu = jnp.mean(x, axis=-1, keepdims=True)
            var = jnp.var(x, axis=-1, keepdims=True)
            return (x - mu) * jax.lax.rsqrt(var + EPS) * g + b
        b, s, h = x.shape
        hn = _layernorm(x, ln1_g, ln1_b)
        q = (hn @ wq + bq).reshape(b, s, NH, D).transpose(0, 2, 1, 3)
        k = (hn @ wk + bk).reshape(b, s, NH, D).transpose(0, 2, 1, 3)
        v = (hn @ wv + bv).reshape(b, s, NH, D).transpose(0, 2, 1, 3)
        scores = jnp.einsum('bhqd,bhkd->bhqk', q, k) / jnp.sqrt(jnp.float32(D))
        attn = jax.nn.softmax(scores, axis=-1)
        o = jnp.einsum('bhqk,bhkd->bhqd', attn, v)
        o = o.transpose(0, 2, 1, 3).reshape(b, s, h)
        x = x + (o @ wo + bo)
        hn2 = _layernorm(x, ln2_g, ln2_b).reshape(-1, h)
        logits = hn2 @ gate_w + gate_b
        idx = jnp.argmax(logits, axis=-1)
        mid = jax.nn.relu(jnp.einsum('th,ehf->etf', hn2, w1) + b1[:, None, :])
        y = jnp.einsum('etf,efh->eth', mid, w2) + b2[:, None, :]
        moe = y[idx, jnp.arange(hn2.shape[0])]
        return x + moe.reshape(b, s, h)
    x = L0_attn_hidden_states
    x = _layernorm(x + _L0_attn_ref(x, L0_attn_Wq, L0_attn_bq, L0_attn_Wk, L0_attn_bk, L0_attn_Wv, L0_attn_bv), axis=-1)
    x = _layernorm(x + _L0_ffn_ref(x, L0_ffn_ln1_g, L0_ffn_ln1_b, L0_ffn_ln2_g, L0_ffn_ln2_b, L0_ffn_wq, L0_ffn_bq, L0_ffn_wk, L0_ffn_bk, L0_ffn_wv, L0_ffn_bv, L0_ffn_wo, L0_ffn_bo, L0_ffn_gate_w, L0_ffn_gate_b, L0_ffn_w1, L0_ffn_b1, L0_ffn_w2, L0_ffn_b2), axis=-1)
    return x

_drawn_inputs = setup_inputs


def setup_inputs(seed=0):
    import zlib

    import numpy as np

    out = dict(_drawn_inputs(seed))
    spreads = {'L0_ffn_ln1_g': (1.0, 0.6),
     'L0_ffn_ln1_b': (0.0, 0.8),
     'L0_ffn_ln2_g': (1.0, 0.2),
     'L0_ffn_ln2_b': (0.0, 0.429),
     'L0_ffn_bq': (0.0, 0.8),
     'L0_ffn_bk': (0.0, 0.8),
     'L0_ffn_bv': (0.0, 0.514),
     'L0_ffn_bo': (0.0, 0.1),
     'L0_ffn_gate_b': (0.0, 0.1),
     'L0_ffn_b1': (0.0, 0.532),
     'L0_ffn_b2': (0.0, 0.1)}
    factors = {'L0_attn_bq': 4.509,
     'L0_attn_bk': 8.0,
     'L0_ffn_wq': 8.0,
     'L0_ffn_wk': 8.0,
     'L0_ffn_wv': 7.449,
     'L0_ffn_wo': 3.544}
    for name, (base, spread) in spreads.items():
        noise = np.random.default_rng([zlib.crc32(name.encode()), seed]).standard_normal(out[name].shape)
        drawn = base * np.exp(spread * noise) if base else spread * noise
        out[name] = jnp.asarray(drawn.astype(out[name].dtype))
    for name, factor in factors.items():
        out[name] = (out[name] * factor).astype(out[name].dtype)
    return out
```

```python
from contextlib import ExitStack

import numpy as np

import concourse.bass as bass
from concourse import mybir

ALU = mybir.AluOpType
ACT = mybir.ActivationFunctionType
AX_X = mybir.AxisListType.X
F32 = mybir.dt.float32
BF16 = mybir.dt.bfloat16

P = 128
B, SEQ, HS = 2, 1024, 128
H, D = 16, 8
BLK = 64
TT = SEQ // P
G = B * TT
E, F = 8, 512
FC = F // P
PAIRS = H // 2
UNITS = B * PAIRS
UB = 4
SLOT = 64
MROW = 6 * D
SCALE = float(np.float32(1.0 / np.sqrt(D)))
EPS = 1e-5
Q_HI, Q_MID, Q_LO = (0, 3, 1), (3, 2, 1), (5, 1, 1)
K_HI, K_HI2, K_MID, K_LO = (0, 2, 3), (5, 1, 1), (1, 2, 3), (2, 1, 1)


def block_col(i):
    return BLK * {0: 0, SEQ // BLK - 1: 1, 1: SEQ // BLK - 1}.get(i, i)


def mm(bank, rows, col, left, right):
    return dict(bank=bank, rows=rows, col=col, left=left, right=right)


ALL, LOW, UPP = (0, P), (0, BLK), (BLK, P)


class Layer:
    pass


def full_layer():
    L = Layer()
    L.slots = 2 * TT
    L.max_steps = [
        dict(h=h, mms=[mm(k, ALL, 0, (t * P, P), (k * 512, 512)) for k in range(2)],
             view=("flat", 1024), out=(h * TT + t, 1, 1))
        for h in range(2) for t in range(TT)]
    L.max_slot = list(range(2 * TT))
    L.exp_tiles = [
        dict(n=512, mms=[(h, mm(0, ALL, 0, (kt * P, P), (half * 512, 512)))])
        for kt in range(TT) for h in range(2) for half in range(2)]
    L.ring = 8
    L.av_groups = [
        dict(last=4 * kt + 3,
             mms=[(h, half, 4 * kt + 2 * h + half, (0, 512), "full", kt, 0)
                  for h in range(2) for half in range(2)])
        for kt in range(TT)]
    L.av_slot = [2 * g + 3 for g in range(TT)]
    L.kinds = ["full"]
    L.at = dict(MT=4, OT=6, K=9, Q=13)
    L.cut = 7
    return L


def block_layer():
    L = Layer()
    L.slots = 7
    L.max_steps = []
    for h in range(2):
        L.max_steps.append(dict(h=h, mms=[mm(k, ALL, 0, (0, P), (k * 512, 512)) for k in range(2)],
                                view=("flat", 1024), out=(h * TT, 1, 1)))
        for j0 in (1, 3, 5):
            mms = []
            for k in range(2):
                j = j0 + k
                mms += [mm(k, ALL, 0, (j * P, P), (0, P)),
                        mm(k, ALL, P, (j * P, P), (j * P, P)),
                        mm(k, LOW, 2 * P, (j * P, BLK), (block_col(2 * j - 1), BLK)),
                        mm(k, UPP, 2 * P, (j * P + BLK, BLK), (block_col(2 * j + 2), BLK))]
            L.max_steps.append(dict(h=h, mms=mms, view=("banks", 320), out=(h * TT + j0, 2, 1)))
    t7 = (TT - 1) * P
    mms = []
    for h in range(2):
        mms += [(h, mm(h, ALL, 0, (t7, P), (0, P))),
                (h, mm(h, LOW, P, (t7, BLK), (block_col(13), P))),
                (h, mm(h, UPP, P, (t7 + BLK, BLK), (block_col(1), BLK))),
                (h, mm(h, UPP, P + BLK, (t7 + BLK, BLK), (block_col(2), BLK)))]
    L.max_steps.append(dict(h=None, mms=mms, view=("banks", 256), out=(TT - 1, 2, TT)))
    L.max_slot = [m * 7 // 9 for m in range(9)]

    def single(j, col):
        return [mm(0, LOW, col, (block_col(2 * j + 2), BLK), (j * P + BLK, BLK)),
                mm(0, UPP, col, (block_col(2 * j - 1), BLK), (j * P, BLK))]

    def single_v(h, e, j, col):
        q0, q1 = j * P, j * P + BLK
        return [(h, q0 // 512, e, (col, BLK), "upp", block_col(2 * j - 1) // P, q0 % 512),
                (h, q1 // 512, e, (col, BLK), "low", block_col(2 * j + 2) // P, q1 % 512)]

    t1, t6 = block_col(2) // P, block_col(13) // P
    tiles, groups = [], []
    for kind in range(6):
        group = dict(last=2 * kind + 1, mms=[])
        per_head = []
        for h in range(2):
            e, v = 2 * kind + h, []
            if kind < 2:
                ts = range(4 * kind, 4 * kind + 4)
                mms = [mm(0, ALL, i * P, (t * P, P), (0, P)) for i, t in enumerate(ts)]
                v = [(h, 0, e, (i * P, P), "full", t, 0) for i, t in enumerate(ts)]
                n = 512
            elif kind == 2:
                mms = [mm(0, ALL, 0, (0, P), (P, 512))]
                v = [(h, 0, e, (0, 384), "full", 0, P), (h, 1, e, (384, P), "full", 0, 0)]
                n = 512
            elif kind == 3:
                mms = [mm(0, ALL, 0, (0, P), (640, 384)),
                       mm(0, LOW, 384, (block_col(14), BLK), (t7, BLK)),
                       mm(0, UPP, 384, (block_col(13), BLK), (t7, BLK)),
                       mm(0, LOW, 448, (block_col(2), BLK), (t7 + BLK, BLK)),
                       mm(0, UPP, 448, (block_col(1), BLK), (t7 + BLK, BLK))]
                v = [(h, 1, e, (0, 384), "full", 0, P),
                     (h, 1, e, (384, BLK), "low", TT - 1, 384), (h, 1, e, (384, BLK), "upp", t6, 384),
                     (h, 1, e, (448, BLK), "low", t1, 448), (h, 1, e, (448, BLK), "upp", TT - 1, 448)]
                n = 512
            elif kind == 4:
                mms = [mm(0, ALL, (j - 1) * P, (j * P, P), (j * P, P)) for j in range(1, 5)]
                v = [(h, j // 4, e, ((j - 1) * P, P), "full", j, j % 4 * P) for j in range(1, 5)]
                n = 512
            else:
                mms = [mm(0, ALL, (j - 5) * P, (j * P, P), (j * P, P)) for j in (5, 6)]
                v = [(h, 1, e, ((j - 5) * P, P), "full", j, j % 4 * P) for j in (5, 6)]
                for j in range(1, 5):
                    mms += single(j, 256 + (j - 1) * BLK)
                    v += single_v(h, e, j, 256 + (j - 1) * BLK)
                n = 512
            tiles.append(dict(n=n, mms=[(h, m) for m in mms]))
            per_head.append(v)
        for a, b in zip(*per_head):
            group["mms"] += [a, b]
        groups.append(group)
    mms, per_head = [], []
    for h in range(2):
        v = []
        for j in (5, 6):
            col = h * P + (j - 5) * BLK
            mms += [(h, m) for m in single(j, col)]
            v += single_v(h, 12, j, col)
        per_head.append(v)
    tiles.append(dict(n=2 * P, mms=mms))
    groups.append(dict(last=12, mms=[x for pair in zip(*per_head) for x in pair]))
    L.exp_tiles, L.av_groups = tiles, groups
    L.ring = len(tiles)
    L.av_slot = [g + 1 for g in range(7)]
    L.kinds = ["full", "low", "upp"]
    L.at = dict(MT=2, OT=3, K=4, Q=6)
    L.cut = 11
    return L


def mark_ends(L):
    flat = [(g, i, m[:2]) for g, gr in enumerate(L.av_groups) for i, m in enumerate(gr["mms"])]
    first, last = {}, {}
    for g, i, key in flat:
        first.setdefault(key, (g, i))
        last[key] = (g, i)
    for g, gr in enumerate(L.av_groups):
        gr["mms"] = [m + (first[m[:2]] == (g, i), last[m[:2]] == (g, i)) for i, m in enumerate(gr["mms"])]
    return L


def plan(L):
    S, acts = L.slots, []
    for u in range(UNITS):
        acts += [(u * S + e // 2, 0, "EXP", u, e) for e in range(len(L.exp_tiles))]
        acts += [((u - 2) * S + s, 1, "MAX", u, m) for m, s in enumerate(L.max_slot)]
        acts += [(u * S + s, 2, "AV", u, g) for g, s in enumerate(L.av_slot)]
        acts += [(u * S + L.av_slot[-1], 3, "OE", u, 0)]
        acts += [((u - 1) * S + L.at["MT"], 4, "MT", u, 0), ((u + 1) * S + L.at["OT"], 5, "OT", u, 0)]
        acts += [((u - 1) * S + L.av_slot[-1] - S + 1, 8, "V", u, 0)]
        acts += [((u - 3) * S + L.at["K"], 6, "K", u, 0), ((u - 3) * S + L.at["Q"], 7, "Q", u, 0)]
    acts.sort()
    shared, before = {}, None
    for _, _, kind, u, _ in acts:
        if kind in ("K", "Q", "MT", "OT"):
            shared[kind, u] = before
            before = (kind, u)
    rounds = (UNITS - UB) // UB
    lo, hi = L.cut, L.cut + UB * S
    body = [a for a in acts if lo <= a[0] < hi]
    for r in range(1, rounds):
        again = [(t + r * UB * S, p, k, u + r * UB, x) for t, p, k, u, x in body]
        assert again == [a for a in acts if lo + r * UB * S <= a[0] < hi + r * UB * S]
    head = [a for a in acts if a[0] < lo]
    tail = [a for a in acts if a[0] >= lo + rounds * UB * S]
    return [[a[2:] for a in part] for part in (head, body, tail)], rounds, shared


def build(nc, x, Wq, bq, Wk, bk, Wv, bv, ln1_g, ln1_b, ln2_g, ln2_b, fwq, fbq, fwk, fbk, fwv, fbv, fwo, fbo,
          gate_w, gate_b, w1, b1, w2, b2, out):
    LAYERS = [mark_ends(block_layer()), mark_ends(full_layer())]
    PLANS = [plan(L) for L in LAYERS]
    with ExitStack() as ctx:
        def sb(name, shape, dt=F32):
            return ctx.enter_context(nc.sbuf_tensor(name, shape, dt))

        def pb(name, shape, dt=F32):
            return ctx.enter_context(nc.psum_tensor(name, shape, dt))

        def sem(name):
            return ctx.enter_context(nc.semaphore(name))

        X = sb("X", [P, G, HS])
        X1 = sb("X1", [P, G, HS])
        CTX = sb("CTX", [P, TT, B, H * D])
        XT = sb("XT", [P, G * P])
        QKV = sb("QKV", [P, G, 2 * HS])
        VST = sb("VST", [P, TT, B, H * D])
        QK = sb("QK", [P, 2, TT, B, H, SLOT], BF16)
        WQKV = sb("WQKV", [P, 3 * HS])
        WF = sb("WF", [P, 3 * HS])
        BIAS = sb("BIAS", [P, 2, 3 * HS])
        WO = sb("WO", [P, HS])
        GW = sb("GW", [P, E])
        ROWS = sb("ROWS", [P, 5, HS])
        GB = sb("GB", [P, E])
        B1R = sb("B1R", [E * FC, P])
        B1T = sb("B1T", [P, E * FC])
        B2 = sb("B2", [E, HS])
        IDF = sb("IDF", [P, P])
        IDB = sb("IDB", [P, P], BF16)
        QT = [sb(f"QT{i}", [P, SEQ], BF16) for i in range(UB)]
        KT = [sb(f"KT{i}", [P, 2, SEQ], BF16) for i in range(UB)]
        VB = [sb(f"VB{i}", [P, 3, TT, 2, 32]) for i in range(2)]
        PR = sb("PR", [P, 13, 512])
        NM = [sb(f"NM{i}", [P, 2 * TT]) for i in range(2)]
        NR = [sb(f"NR{i}", [P, 2 * TT]) for i in range(2)]
        MS = [sb(f"MS{i}", [P, 2, 3, TT], BF16) for i in range(2)]
        MT = [sb(f"MT{i}", [6 * TT, P], BF16) for i in range(2)]
        OS = sb("OS", [P, 512])
        WRAW = OS[:, 0:3 * HS].rearrange("p (i c) -> p i c", i=3)
        RS = sb("RS", [P, 2 * TT])
        ST = sb("ST", [P, G, 6])
        MV = sb("MV", [P, G, 2])
        VE = sb("VE", [P, G])
        SD = sb("SD", [P, G])
        RD = sb("RD", [P, G])
        LG = sb("LG", [P, G, E])
        LE = sb("LE", [P, G, E])
        LM = sb("LM", [P, G])
        OH = sb("OH", [P, G, E])
        OHT = VST[0:E].rearrange("p t b c -> p (t b c)")
        RANK = sb("RANK", [P, E])
        W1 = [sb(f"W1_{i}", [P, F]) for i in range(2)]
        W2 = [sb(f"W2_{i}", [P, FC, HS]) for i in range(2)]
        MID = [PR[:, 4 * i:4 * i + 4, :] for i in range(2)]
        MOE = CTX[:].rearrange("p t b c -> p (t b) c")

        HN2 = QKV[:].rearrange("p g c -> p (g c)")[:, 0:G * HS].rearrange("p (g c) -> p g c", g=G)

        PM = [pb(f"PM{i}", [P, 1024]) for i in range(2)]
        PE = [pb(f"PE{i}", [P, 512]) for i in range(2)]
        PO = pb("PO", [P, 512])
        PX = pb("PX", [P, 512])
        PXB = PX[:].bitcast(BF16)
        PMR = [PM[i // 2][:, 512 * (i % 2):512 * (i % 2) + 512] for i in range(4)]

        s_x = sem("s_x"); s_w = sem("s_w"); s_small = sem("s_small"); s_out = sem("s_out")
        s_ident = sem("s_ident"); s_init = sem("s_init"); s_const = sem("s_const"); s_rank = sem("s_rank")
        s_wt = sem("s_wt"); s_wready = sem("s_wready"); s_bscaled = sem("s_bscaled")
        s_src = sem("s_src")
        s_xt = sem("s_xt"); s_xte = sem("s_xte")
        s_proj = sem("s_proj"); s_proje = sem("s_proje")
        s_hi = sem("s_hi"); s_rem = sem("s_rem"); s_mid = sem("s_mid"); s_lo = sem("s_lo")
        s_trans = sem("s_trans"); s_qk = sem("s_qk")
        s_maxmm = sem("s_maxmm"); s_max = sem("s_max"); s_split = sem("s_split")
        s_mt = sem("s_mt"); s_mte = sem("s_mte"); s_mrow = sem("s_mrow")
        s_sc = sem("s_sc"); s_exp = sem("s_exp"); s_v = sem("s_v")
        s_av = sem("s_av"); s_oe = sem("s_oe"); s_ot = sem("s_ot"); s_rs = sem("s_rs"); s_ctx = sem("s_ctx")
        s_dve = sem("s_dve")
        s_var = sem("s_var"); s_std = sem("s_std")
        s_wo = sem("s_wo"); s_gate = sem("s_gate"); s_oh = sem("s_oh"); s_oht = sem("s_oht")
        s_ohte = sem("s_ohte"); s_b2m = sem("s_b2m"); s_b2e = sem("s_b2e")
        s_hid = sem("s_hid"); s_mida = sem("s_mida"); s_midv = sem("s_midv"); s_y = sem("s_y"); s_ye = sem("s_ye")
        s_we = [sem(f"s_we{i}") for i in range(2)]
        s_fin = sem("s_fin")

        NCONST = UB + 3 * TT + E
        NX = [len(L.exp_tiles) for L in LAYERS]
        NMX = [len(L.max_steps) for L in LAYERS]
        NAV = [len(L.av_groups) for L in LAYERS]
        BX = [0, UNITS * NX[0]]
        BM = [0, UNITS * NMX[0]]
        BA = [0, UNITS * NAV[0]]
        BU = [0, UNITS]

        def wait(eng, s, value):
            if not (isinstance(value, int) and value <= 0):
                eng.wait_ge(s, value)

        def run(eng, li, do):
            (head, body, tail), rounds, _ = PLANS[li]
            for kind, u, k in head:
                do(kind, u, u, k)
            with eng.Fori(0, rounds) as r:
                for kind, u, k in body:
                    do(kind, u, r * UB + u, k)
            for kind, u, k in tail:
                do(kind, u + 0, u, k)

        def unit_cols(t, u, n):
            return t[:, bass.ds(u * n, n)]

        block = ctx.enter_context(nc.Block())

        @block.sync
        def _(sp):
            for b in range(B):
                xb = x[b]
                g = b * TT
                sp.dma_start(X[:, g + 1:g + 7, :], xb[P:7 * P, :].rearrange("(j p) c -> p j c", p=P)).then_inc(s_x, 16)
                for t, half, blk in ((0, 0, 0), (0, 1, 15), (7, 0, 14), (7, 1, 1)):
                    sp.dma_start(X[half * BLK:(half + 1) * BLK, g + t, :],
                                 xb[blk * BLK:(blk + 1) * BLK, :]).then_inc(s_x, 16)
            for i, w in enumerate((Wq, Wk, Wv)):
                sp.dma_start(WRAW[:, i, :], w[:, :]).then_inc(s_w, 16)
            for i, v in enumerate((bq, bk, bv, fbq, fbk, fbv)):
                sp.dma_start(BIAS[:, i // 3, (i % 3) * HS:(i % 3 + 1) * HS], v.partition_broadcast(P)).then_inc(s_w, 16)
            for i, w in enumerate((fwq, fwk, fwv)):
                sp.dma_start(WF[:, i * HS:(i + 1) * HS], w[:, :]).then_inc(s_small, 16)
            sp.dma_start(WO[:], fwo[:, :]).then_inc(s_small, 16)
            sp.dma_start(GW[:], gate_w[:, :]).then_inc(s_small, 16)
            sp.dma_start(GB[:], gate_b.partition_broadcast(P)).then_inc(s_small, 16)
            for i, v in enumerate((ln1_g, ln1_b, ln2_g, ln2_b, fbo)):
                sp.dma_start(ROWS[:, i, :], v.partition_broadcast(P)).then_inc(s_small, 16)
            sp.dma_start(B1R[:], b1.rearrange("e (c f) -> (e c) f", f=P)).then_inc(s_small, 16)
            sp.dma_start(B2[:], b2[:, :]).then_inc(s_small, 16)
            for e in range(2):
                sp.dma_start(W1[e][:], w1[e]).then_inc(s_we[e], 16)
                sp.dma_start(W2[e][:], w2[e].rearrange("(c f) n -> f c n", f=P)).then_inc(s_we[e], 16)

            for li in range(2):
                def do(kind, u0, u, k, li=li):
                    if kind == "MT":
                        sp.wait_ge(s_mte, BU[li] + u + 1)
                        for h in range(2):
                            for part in range(3):
                                r = (h * 3 + part) * TT
                                row = h * SLOT + MROW + part
                                sp.dma_start(QT[u0 % UB][row:row + 1, :].rearrange("o (t q) -> o t q", t=TT),
                                             MT[u0 % 2][r:r + TT, :]).then_inc(s_mrow, 16)
                run(sp, li, do)

            with sp.Fori(0, E // 2 - 1) as r:
                for i in range(2):
                    e = r * 2 + (i + 2)
                    sp.wait_ge(s_y, r * (2 * 4) + (4 * (i + 1) + 2))
                    sp.dma_start(W1[i][:], w1[bass.ds(e, 1)].rearrange("o h f -> (o h) f")).then_inc(s_we[i], 16)
                    sp.dma_start(W2[i][:], w2[bass.ds(e, 1)].rearrange("o (c f) n -> (o f) c n", f=P)).then_inc(s_we[i], 16)

            for b in range(B):
                g = b * TT
                sp.wait_ge(s_fin, (b + 1) * TT)
                ob = out[b]
                sp.dma_start(ob[P:7 * P, :].rearrange("(j p) c -> p j c", p=P), X1[:, g + 1:g + 7, :]).then_inc(s_out, 16)
                for t, half, blk in ((0, 0, 0), (0, 1, 15), (7, 0, 14), (7, 1, 1)):
                    sp.dma_start(ob[blk * BLK:(blk + 1) * BLK, :],
                                 X1[half * BLK:(half + 1) * BLK, g + t, :]).then_inc(s_out, 16)
            sp.wait_ge(s_out, 16 * 5 * B)

        @block.gpsimd
        def _(pool):
            nc.gpsimd.memset(IDF[:], 0.0).then_inc(s_rank, 1)
            nc.gpsimd.memset(IDB[:], 0.0).then_inc(s_rank, 1)
            pool.wait_ge(s_rank, 2)
            for t in (IDF, IDB):
                nc.gpsimd.affine_select(out=t[:], in_=t[:], compare_op=ALU.not_equal, fill=1.0, base=0,
                                        pattern=[[-1, P]], channel_multiplier=1).then_inc(s_ident, 1)
            pool.wait_ge(s_ident, 2)
            n = 0
            for i in range(2):
                for kind, rows in enumerate((ALL, ALL, LOW, UPP)):
                    if kind == 0:
                        nc.gpsimd.memset(VB[i][:], 0.0).then_inc(s_init, 1)
                    else:
                        nc.gpsimd.memset(VB[i][rows[0]:rows[1], kind - 1, :, :, D:D + 1], 1.0).then_inc(s_init, 1)
                    n += 1
                    pool.wait_ge(s_init, n)

            for li, L in enumerate(LAYERS):
                def do(kind, u0, u, k, li=li, L=L):
                    if kind == "V":
                        if u0 == 0 and k == 0 and isinstance(u, int):
                            pool.wait_ge(s_proje, 2 * G * (li + 1))
                        wait(pool, s_av, (u - 1) * NAV[li] + BA[li] if not isinstance(u, int) or u >= 2
                             else BA[li])
                        src = VST[:].rearrange("p t b c -> p t (b c)")[:, :, bass.ds(u * 2 * D, 2 * D)] \
                            .rearrange("p t (h d) -> p t h d", h=2)
                        pool.nop(nofuse=True)
                        for i, kd in enumerate(L.kinds):
                            lo, hi = {"full": ALL, "low": LOW, "upp": UPP}[kd]
                            nc.gpsimd.tensor_copy(VB[u0 % 2][lo:hi, i, :, :, 0:D], src[lo:hi]).then_inc(s_v, 1)
                            pool.wait_ge(s_v, (3 * UNITS if li else 0) + u * len(L.kinds) + (i + 1))
                            pool.nop(nofuse=True)
                    if kind == "MT":
                        a, r, m = NM[u0 % 2], NR[u0 % 2], MS[u0 % 2]
                        a3 = a[:].rearrange("p (h t) -> p h t", h=2)
                        r3 = r[:].rearrange("p (h t) -> p h t", h=2)
                        c = BU[li] * 4 + u * 4
                        pool.wait_ge(s_max, BM[li] + (u + 1) * NMX[li])
                        wait(pool, s_mt, BU[li] + u - 1)
                        pool.nop(nofuse=True)
                        nc.gpsimd.tensor_copy(m[:, :, 0, :], a3).then_inc(s_split, 1)
                        pool.wait_ge(s_split, c + 1)
                        nc.gpsimd.tensor_tensor(r3, a3, m[:, :, 0, :], ALU.subtract).then_inc(s_split, 1)
                        pool.wait_ge(s_split, c + 2)
                        pool.nop(nofuse=True)
                        nc.gpsimd.tensor_copy(m[:, :, 1, :], r3).then_inc(s_split, 1)
                        pool.wait_ge(s_split, c + 3)
                        nc.gpsimd.tensor_tensor(m[:, :, 2, :], r3, m[:, :, 1, :], ALU.subtract).then_inc(s_split, 1)
                run(pool, li, do)

        @block.scalar
        def _(act):
            act.wait_ge(s_wt, 3)
            nc.scalar.mul(WQKV[:, 0:HS], PX[:, 0:HS], SCALE).then_inc(s_wready, 1)
            nc.scalar.copy(WQKV[:, HS:3 * HS], PX[:, HS:3 * HS]).then_inc(s_wready, 1)
            act.wait_ge(s_w, 16 * 9)
            for i in range(2):
                nc.scalar.mul(BIAS[:, i, 0:HS], BIAS[:, i, 0:HS], SCALE).then_inc(s_bscaled, 1)

            def project(li):
                for q in range(G // 4):
                    act.wait_ge(s_xt, 4 * li + q + 1)
                    nc.scalar.copy(XT[:, q * 512:(q + 1) * 512], PE[q % 2][:]).then_inc(s_xte, 1)
                for q in range(G // 4):
                    b, t0 = divmod(4 * q, TT)
                    act.wait_ge(s_proje, 2 * (G * li + 4 * q + 4))
                    src = [QKV[:, 4 * q:4 * q + 4, w * HS:(w + 1) * HS] for w in range(2)]
                    for w, (s0, n, st) in ((0, Q_HI), (1, K_HI), (1, K_HI2)):
                        for t in range(4):
                            o = QK[:, w, t0 + t, b, :, :]
                            o = o[:, :, 0:MROW].rearrange("p h (s d) -> p h s d", d=D)[:, :, s0:s0 + (n - 1) * st + 1:st, :]
                            i = src[w][:, t, :].rearrange("p (h d) -> p h d", d=D).unsqueeze(2).broadcast_to([P, H, n, D])
                            nc.scalar.copy(o, i).then_inc(s_hi, 1)
                    act.wait_ge(s_rem, 8 * (4 * li + q + 1))
                    for w, (s0, n, st) in ((0, Q_MID), (1, K_MID)):
                        for t in range(4):
                            o = QK[:, w, t0 + t, b, :, :]
                            o = o[:, :, 0:MROW].rearrange("p h (s d) -> p h s d", d=D)[:, :, s0:s0 + (n - 1) * st + 1:st, :]
                            i = src[w][:, t, :].rearrange("p (h d) -> p h d", d=D).unsqueeze(2).broadcast_to([P, H, n, D])
                            nc.scalar.copy(o, i).then_inc(s_mid, 1)

            for li, L in enumerate(LAYERS):
                if li == 1:
                    for n in range(2):
                        act.wait_ge(s_var, n + 1)
                        nc.scalar.activation(SD[:], VE[:], ACT.Sqrt).then_inc(s_std, 1)
                    act.wait_ge(s_small, 16 * 13)
                    nc.scalar.mul(WF[:, 0:HS], WF[:, 0:HS], SCALE).then_inc(s_wready, 1)
                project(li)

                def do(kind, u0, u, k, li=li, L=L):
                    if kind == "K":
                        wait(act, s_sc, BX[li] + (u - UB + 1) * NX[li] if not isinstance(u, int) or u >= UB
                             else BX[li])
                        act.wait_ge(s_trans, 2 * BU[li] + 2 * u + 1)
                        for h in range(2):
                            r = slice(h * SLOT, (h + 1) * SLOT)
                            nc.scalar.copy(KT[u0 % UB][r, h, :], PXB[r, :]).then_inc(s_qk, 1)
                    if kind == "Q":
                        act.wait_ge(s_trans, 2 * BU[li] + 2 * u + 2)
                        nc.scalar.copy(QT[u0 % UB][:], PXB).then_inc(s_qk, 1)
                    if kind == "EXP":
                        n = L.exp_tiles[k]["n"]
                        count = BX[li] + u * NX[li] + k
                        act.wait_ge(s_sc, count + 1)
                        e = k - L.ring
                        du = 0
                        while e < 0:
                            e += NX[li]
                            du -= 1
                        g = [i for i, gr in enumerate(L.av_groups) if gr["last"] >= e][0]
                        if li == 1 and isinstance(u, int) and u == 0 and k == 0:
                            act.wait_ge(s_av, BA[1])
                        if not isinstance(u, int) or u + du >= 0:
                            act.wait_ge(s_av, BA[li] + (u + du) * NAV[li] + g + 1)
                        nc.scalar.activation(PR[:, k % L.ring, 0:n], PE[(u0 * NX[li] + k) % 2][:, 0:n],
                                             ACT.Exp).then_inc(s_exp, 1)
                run(act, li, do)

            for n in range(2):
                for q in range(G // 4):
                    act.wait_ge(s_xt, 8 + 4 * n + q + 1)
                    nc.scalar.copy(XT[:, q * 512:(q + 1) * 512], PE[q % 2][:]).then_inc(s_xte, 1)
                if n == 0:
                    act.wait_ge(s_wt, 4)
                    nc.scalar.copy(B1T[:], PX[:, 0:E * FC]).then_inc(s_wready, 1)
                    act.wait_ge(s_var, 3)
                    nc.scalar.activation(SD[:], VE[:], ACT.Sqrt).then_inc(s_std, 1)
            for q in range(G // 4):
                act.wait_ge(s_oht, q + 1)
                nc.scalar.copy(OHT[:, q * 512:(q + 1) * 512], PE[q % 2][0:E, :]).then_inc(s_ohte, 1)
            act.wait_ge(s_wready, 4)
            act.nop(nofuse=True).then_inc(s_mida, 1)
            with act.Fori(0, E // 2) as r:
                for i in range(2):
                    for c in range(4):
                        for f in (0, 2):
                            n = (r * 2 + i) * 4 + c
                            act.wait_ge(s_hid, n * 4 + f + 1)
                            act.wait_ge(s_y, n + 1)
                            act.nop(nofuse=True)
                            nc.scalar.activation(MID[c % 2][:, f, :], PMR[f], ACT.Relu,
                                                 bias=B1T[:, bass.ds((r * 2 + i) * FC + f, 1)]).then_inc(s_mida, 1)
            act.wait_ge(s_var, 4)
            nc.scalar.activation(SD[:], VE[:], ACT.Sqrt).then_inc(s_std, 1)

        @block.vector
        def _(dve):
            chain = [0]

            def link(ins):
                chain[0] += 1
                ins.then_inc(s_dve, 1)
                dve.wait_ge(s_dve, chain[0])

            def step(ins):
                chain[0] += 1
                ins.then_inc(s_dve, 1)

            for i in range(UB):
                nc.vector.memset(KT[i][:], 0.0).then_inc(s_const, 1)
            for w in range(2):
                for t in range(TT):
                    nc.vector.memset(QK[:, w, t, :, :, MROW:SLOT], 0.0).then_inc(s_const, 1)
            dve.wait_ge(s_const, UB + 2 * TT)
            for t in range(TT):
                nc.vector.memset(QK[:, 1, t, :, :, MROW:MROW + 3], 1.0).then_inc(s_const, 1)
            for e in range(E):
                nc.vector.memset(RANK[:, e:e + 1], float(E - e)).then_inc(s_const, 1)
            dve.wait_ge(s_const, NCONST)

            def project(li):
                bias = BIAS[:, li, :]
                dve.wait_ge(s_bscaled, 2)
                for g in range(G):
                    b, t = divmod(g, TT)
                    ps = PMR[g % 4]
                    dve.wait_ge(s_proj, G * li + g + 1)
                    if li == 1 and g == 0:
                        dve.wait_ge(s_v, 3 * UNITS)
                    nc.vector.tensor_tensor(QKV[:, g, :], ps[:, 0:2 * HS], bias[:, 0:2 * HS], ALU.add).then_inc(s_proje, 1)
                    nc.vector.tensor_tensor(VST[:, t, b, :], ps[:, 2 * HS:3 * HS], bias[:, 2 * HS:3 * HS],
                                            ALU.add).then_inc(s_proje, 1)
                for q in range(G // 4):
                    b, t0 = divmod(4 * q, TT)
                    dve.wait_ge(s_proje, 2 * (G * li + 4 * q + 4))
                    dve.wait_ge(s_hi, 12 * (4 * li + q + 1))
                    for t in range(4):
                        for w in range(2):
                            s = QKV[:, 4 * q + t, w * HS:(w + 1) * HS].rearrange("p (h d) -> p h d", d=D)
                            nc.vector.tensor_tensor(s, s, QK[:, w, t0 + t, b, :, 0:D], ALU.subtract).then_inc(s_rem, 1)
                    dve.wait_ge(s_mid, 8 * (4 * li + q + 1))
                    for t in range(4):
                        for w, lo, md in ((0, Q_LO[0], Q_MID[0]), (1, K_LO[0], K_MID[0])):
                            s = QKV[:, 4 * q + t, w * HS:(w + 1) * HS].rearrange("p (h d) -> p h d", d=D)
                            nc.vector.tensor_tensor(QK[:, w, t0 + t, b, :, lo * D:(lo + 1) * D], s,
                                                    QK[:, w, t0 + t, b, :, md * D:(md + 1) * D],
                                                    ALU.subtract).then_inc(s_lo, 1)

            def norm(src, dst, n, fin=None):
                for g in range(G):
                    step(nc.vector.bn_stats(ST[:, g, :], src[:, g, :]))
                dve.wait_ge(s_dve, chain[0])
                for g in range(G):
                    step(nc.vector.bn_aggr(MV[:, g, :], ST[:, g, :]))
                dve.wait_ge(s_dve, chain[0])
                nc.vector.tensor_scalar(VE[:], MV[:, :, 1], EPS, None, ALU.add).then_inc(s_var, 1)
                dve.wait_ge(s_std, n)
                link(nc.vector.reciprocal(RD[:], SD[:]))
                for g in range(G):
                    ins = nc.vector.tensor_scalar(dst[:, g, :], src[:, g, :], MV[:, g, 0:1], RD[:, g:g + 1],
                                                  ALU.subtract, ALU.mult)
                    if fin is None:
                        step(ins)
                    else:
                        ins.then_inc(fin, 1)
                if fin is None:
                    dve.wait_ge(s_dve, chain[0])

            def affine(dst, k):
                link(nc.vector.tensor_tensor(dst, dst, ROWS[:, k:k + 1, :].broadcast_to([P, G, HS]), ALU.mult))
                nc.vector.tensor_tensor(dst, dst, ROWS[:, k + 1:k + 2, :].broadcast_to([P, G, HS]),
                                        ALU.add).then_inc(s_src, 1)

            for li, L in enumerate(LAYERS):
                if li == 1:
                    dve.wait_ge(s_x, 16 * 10)
                    dve.wait_ge(s_ctx, 2 * UNITS)
                    xv = X[:].rearrange("p (b t) c -> p t b c", b=B)
                    for b in range(B):
                        link(nc.vector.tensor_tensor(xv[:, :, b, :], xv[:, :, b, :], CTX[:, :, b, :], ALU.add))
                    norm(X, X1, 1)
                    norm(X1, X, 2)
                    dve.wait_ge(s_small, 16 * 13)
                    affine(X[:], 0)
                project(li)

                def do(kind, u0, u, k, li=li, L=L):
                    if kind == "MAX":
                        st = L.max_steps[k]
                        pm = PM[(u0 * NMX[li] + k) % 2]
                        dve.wait_ge(s_maxmm, BM[li] + u * NMX[li] + k + 1)
                        if k == 0:
                            wait(dve, s_split, 4 * (BU[li] + u - 1))
                        c, n, step_ = st["out"]
                        o = NM[u0 % 2][:, c:c + (n - 1) * step_ + 1:step_]
                        kind_, w = st["view"]
                        if kind_ == "flat":
                            i = pm[:]
                        else:
                            i = pm[:].rearrange("p (k n) -> p k n", k=2)[:, :, 0:w]
                        nc.vector.tensor_reduce(o, i, AX_X, ALU.max, negate=True).then_inc(s_max, 1)
                    if kind == "MT":
                        dve.wait_ge(s_mt, BU[li] + u + 1)
                        wait(dve, s_mrow, 96 * (BU[li] + u - 1))
                        nc.vector.tensor_copy(MT[u0 % 2][:], PXB[0:6 * TT, 0:P]).then_inc(s_mte, 1)
                    if kind == "OE":
                        dve.wait_ge(s_av, BA[li] + (u + 1) * NAV[li])
                        wait(dve, s_ot, BU[li] + u)
                        nc.vector.tensor_copy(OS[:], PO[:]).then_inc(s_oe, 1)
                    if kind == "OT":
                        px = PX[:].rearrange("p (c h a d) -> p c h a d", c=4, h=2, a=2)
                        rs = RS[:].rearrange("p (c h a) -> p c h a", c=4, h=2)
                        dve.wait_ge(s_ot, BU[li] + u + 1)
                        wait(dve, s_ctx, 2 * (BU[li] + u))
                        nc.vector.reciprocal(RS[:], PX[:].rearrange("p (c d) -> p c d", d=32)[:, :, D]).then_inc(s_rs, 1)
                        dve.wait_ge(s_rs, BU[li] + u + 1)
                        for h in range(2):
                            o = CTX[:].rearrange("p t b c -> p t (b c)")[:, :, bass.ds((u * 2 + h) * D, D)] \
                                .rearrange("p (a c) d -> p c a d", a=2)
                            nc.vector.tensor_tensor(o, px[:, :, h, :, 0:D],
                                                    rs[:, :, h, :].unsqueeze(3).broadcast_to([P, 4, 2, D]),
                                                    ALU.mult).then_inc(s_ctx, 1)
                run(dve, li, do)

            for q in range(G // 4):
                dve.wait_ge(s_wo, q + 1)
                if q == 0:
                    dve.wait_ge(s_xte, 8)
                link(nc.vector.tensor_tensor(X[:, 4 * q:4 * q + 4, :], PMR[q].rearrange("p (t c) -> p t c", t=4),
                                             X1[:, 4 * q:4 * q + 4, :], ALU.add))
            link(nc.vector.tensor_tensor(X[:], X[:], ROWS[:, 4:5, :].broadcast_to([P, G, HS]), ALU.add))
            norm(X, HN2, 3)
            affine(HN2, 2)
            dve.wait_ge(s_gate, 1)
            gb = GB[:].unsqueeze(1).broadcast_to([P, G, E])
            rank = RANK[:].unsqueeze(1).broadcast_to([P, G, E])
            link(nc.vector.tensor_tensor(LG[:], PO[:, 0:G * E].rearrange("p (g e) -> p g e", e=E), gb, ALU.add))
            link(nc.vector.tensor_reduce(LM[:], LG[:], AX_X, ALU.max))
            link(nc.vector.tensor_tensor(LE[:], LG[:], LM[:].unsqueeze(2).broadcast_to([P, G, E]), ALU.is_ge))
            link(nc.vector.tensor_tensor(LE[:], LE[:], rank, ALU.mult))
            link(nc.vector.tensor_reduce(LM[:], LE[:], AX_X, ALU.max))
            nc.vector.tensor_tensor(OH[:], LE[:], LM[:].unsqueeze(2).broadcast_to([P, G, E]),
                                    ALU.is_equal).then_inc(s_oh, 1)
            dve.wait_ge(s_oh, 1)
            for q in range(4):
                dve.wait_ge(s_b2m, q + 1)
                for t in range(4):
                    nc.vector.tensor_copy(MOE[:, 4 * q + t, :], PMR[q][:, t * P:(t + 1) * P]).then_inc(s_ye, 1)
            dve.wait_ge(s_wready, 4)
            ye = PE
            dve.nop(nofuse=True).then_inc(s_midv, 1)
            with dve.Fori(0, E // 2) as r:
                for i in range(2):
                    for c in range(4):
                        n = (r * 2 + i) * 4 + c
                        for f in (1, 3):
                            dve.wait_ge(s_hid, n * 4 + f + 1)
                            dve.wait_ge(s_y, n + 1)
                            nc.vector.tensor_scalar(MID[c % 2][:, f, :], PMR[f],
                                                    B1T[:, bass.ds((r * 2 + i) * FC + f, 1)], 0.0,
                                                    ALU.add, ALU.max).then_inc(s_midv, 1)
                        dve.wait_ge(s_y, n + 3)
                        dve.wait_ge(s_ye, n * 4 + 4)
                        for t in range(4):
                            g = 4 * c + t
                            nc.vector.scalar_tensor_tensor(
                                out=MOE[:, g, :], in0=ye[c % 2][:, t * P:(t + 1) * P],
                                scalar=OH[:, g, bass.ds(r * 2 + i, 1)], in1=MOE[:, g, :],
                                op0=ALU.mult, op1=ALU.add).then_inc(s_ye, 1)
            dve.wait_ge(s_ye, G + E * G)
            link(nc.vector.tensor_tensor(X[:], X[:], X1[:], ALU.add))
            link(nc.vector.tensor_tensor(X[:], X[:], MOE, ALU.add))
            norm(X, X1, 4, s_fin)

        @block.tensor
        def _(pe):
            pe.wait_ge(s_ident, 2)
            pe.wait_ge(s_w, 16 * 9)
            for i in range(3):
                pe.transpose(PX[:, i * P:(i + 1) * P], WRAW[:, i, :], IDF[:]).then_inc(s_wt, 1)

            def transposes(n, src):
                for q in range(G // 4):
                    if q >= 2 or n:
                        pe.wait_ge(s_xte, 4 * n + q - 1)
                    for t in range(4):
                        ins = pe.transpose(PE[q % 2][:, t * P:(t + 1) * P], src(4 * q + t), IDF[:])
                    ins.then_inc(s_xt, 1)

            def project(li):
                if li == 0:
                    pe.wait_ge(s_x, 160)
                else:
                    pe.wait_ge(s_src, 1)
                transposes(li, lambda g: X[:, g, :])
                pe.wait_ge(s_wready, 2 + li)
                w = WQKV if li == 0 else WF
                if li == 1:
                    pe.wait_ge(s_small, 16 * 13)
                for g in range(G):
                    pe.wait_ge(s_xte, 4 * li + g // 4 + 1)
                    if g >= 4:
                        pe.wait_ge(s_proje, 2 * (G * li + g - 3))
                    pe.matmul(PMR[g % 4][:, 0:3 * HS], XT[:, g * P:(g + 1) * P], w[:], start=True,
                              stop=True).then_inc(s_proj, 1)
                pe.wait_ge(s_lo, 8 * 4 * (li + 1))
                pe.wait_ge(s_mid, 8 * 4 * (li + 1))
                if li == 0:
                    pe.wait_ge(s_const, NCONST)

            for li, L in enumerate(LAYERS):
                project(li)
                shared = PLANS[li][2]

                def shared_free(kind, u0, u, li=li, shared=shared):
                    if shared[kind, u0] is None:
                        return
                    k2, u2 = shared[kind, u0]
                    v = u + (u2 - u0)
                    s, value = {"K": (s_qk, 3 * (BU[li] + v) + 2), "Q": (s_qk, 3 * (BU[li] + v) + 3),
                                "MT": (s_mte, BU[li] + v + 1), "OT": (s_ctx, 2 * (BU[li] + v + 1))}[k2]
                    pe.wait_ge(s, value)

                def do(kind, u0, u, k, li=li, L=L):
                    q, kt, vb = QT[u0 % UB], KT[u0 % UB], VB[u0 % 2]
                    if kind in ("K", "Q"):
                        w = 1 if kind == "K" else 0
                        shared_free(kind, u0, u)
                        for t in range(TT):
                            src = QK[:, w, t, :, :, :].rearrange("p b h s -> p (b h s)")[:, bass.ds(u * P, P)]
                            ins = pe.transpose(PXB[:, t * P:(t + 1) * P], src, IDB[:])
                        ins.then_inc(s_trans, 1)
                    if kind == "MAX":
                        st = L.max_steps[k]
                        pm = PM[(u0 * NMX[li] + k) % 2]
                        if k == 0:
                            pe.wait_ge(s_qk, 3 * (BU[li] + u + 1))
                        count = BM[li] + u * NMX[li] + k
                        wait(pe, s_max, count - 1)
                        for item in st["mms"]:
                            h, m = item if isinstance(item, tuple) else (st["h"], item)
                            (r0, r1), (l0, ln), (c0, cn) = m["rows"], m["left"], m["right"]
                            o = m["bank"] * 512 + m["col"]
                            ins = pe.matmul(pm[r0:r1, o:o + cn], q[:, l0:l0 + ln], kt[:, h, c0:c0 + cn],
                                            start=True, stop=True)
                        ins.then_inc(s_maxmm, 1)
                    if kind == "EXP":
                        count = BX[li] + u * NX[li] + k
                        if k == 0:
                            pe.wait_ge(s_mrow, 96 * (BU[li] + u + 1))
                        wait(pe, s_exp, count - 1)
                        ps = PE[(u0 * NX[li] + k) % 2]
                        for h, m in L.exp_tiles[k]["mms"]:
                            (r0, r1), (l0, ln), (c0, cn) = m["rows"], m["left"], m["right"]
                            ins = pe.matmul(ps[r0:r1, m["col"]:m["col"] + cn], kt[:, h, l0:l0 + ln], q[:, c0:c0 + cn],
                                            start=True, stop=True)
                        ins.then_inc(s_sc, 1)
                    if kind == "AV":
                        gr = L.av_groups[k]
                        pe.wait_ge(s_exp, BX[li] + u * NX[li] + gr["last"] + 1)
                        if k == 0:
                            pe.wait_ge(s_v, (3 * UNITS if li else 0) + len(L.kinds) * (u + 1))
                            wait(pe, s_oe, BU[li] + u)
                        for h, half, e, (c0, cn), kd, t, o, first, last in gr["mms"]:
                            r = 64 * h + 32 * half
                            ins = pe.matmul(PO[r:r + 32, o:o + cn], vb[:, L.kinds.index(kd), t, h, :],
                                            PR[:, e % L.ring, c0:c0 + cn], start=first, stop=last,
                                            skip_group_check=True, tile_position=(0, r))
                        ins.then_inc(s_av, 1)
                    if kind == "MT":
                        shared_free(kind, u0, u)
                        pe.wait_ge(s_split, 4 * (BU[li] + u + 1))
                        pe.nop(nofuse=True)
                        pe.transpose(PXB[0:6 * TT, 0:P], MS[u0 % 2][:].rearrange("p h s t -> p (h s t)"),
                                     IDB[:]).then_inc(s_mt, 1)
                    if kind == "OT":
                        shared_free(kind, u0, u)
                        pe.wait_ge(s_oe, BU[li] + u + 1)
                        for c in range(4):
                            ins = pe.transpose(PX[:, c * P:(c + 1) * P], OS[:, c * P:(c + 1) * P], IDF[:])
                        ins.then_inc(s_ot, 1)

                run(pe, li, do)

            pe.wait_ge(s_ctx, 4 * UNITS)
            transposes(2, lambda g: CTX[:, g % TT, g // TT, :])
            pe.wait_ge(s_max, BM[1] + UNITS * NMX[1])
            for g in range(G):
                pe.wait_ge(s_xte, 8 + g // 4 + 1)
                ins = pe.matmul(PMR[g // 4][:, (g % 4) * P:(g % 4 + 1) * P], XT[:, g * P:(g + 1) * P], WO[:],
                                start=True, stop=True)
                if g % 4 == 3:
                    ins.then_inc(s_wo, 1)
            pe.transpose(PX[:, 0:E * FC], B1R[:], IDF[0:E * FC, 0:E * FC]).then_inc(s_wt, 1)
            pe.wait_ge(s_src, 2)
            transposes(3, lambda g: HN2[:, g, :])
            for g in range(G):
                pe.wait_ge(s_xte, 12 + g // 4 + 1)
                ins = pe.matmul(PO[:, g * E:(g + 1) * E], XT[:, g * P:(g + 1) * P], GW[:], start=True, stop=True)
            ins.then_inc(s_gate, 1)
            pe.wait_ge(s_oh, 1)
            for q in range(4):
                if q >= 2:
                    pe.wait_ge(s_ohte, q - 1)
                for t in range(4):
                    ins = pe.transpose(PE[q % 2][0:E, t * P:(t + 1) * P], OH[:, 4 * q + t, :], IDF[:])
                ins.then_inc(s_oht, 1)
            for q in range(4):
                pe.wait_ge(s_ohte, q + 1)
                for t in range(4):
                    g = 4 * q + t
                    ins = pe.matmul(PMR[q][:, t * P:(t + 1) * P], OHT[:, g * P:(g + 1) * P], B2[:], start=True, stop=True)
                ins.then_inc(s_b2m, 1)
            pe.nop(nofuse=True).then_inc(s_y, 2)
            pe.wait_ge(s_ye, G)
            pe.wait_ge(s_wready, 4)
            with pe.Fori(0, E // 2) as r:
                for i in range(2):
                    for c in range(4):
                        n = (r * 2 + i) * 4 + c
                        if c == 0:
                            pe.wait_ge(s_we[i], 32 * r + 32)
                        pe.wait_ge(s_mida, n * 2 + 1)
                        pe.wait_ge(s_midv, n * 2 + 1)
                        for f in range(FC):
                            pe.matmul(PMR[f], W1[i][:, f * P:(f + 1) * P], XT[:, c * 512:(c + 1) * 512],
                                      start=True, stop=True).then_inc(s_hid, 1)
                        pe.wait_ge(s_ye, n * 4 + 12)
                        pe.wait_ge(s_mida, n * 2 + 3)
                        pe.wait_ge(s_midv, n * 2 + 3)
                        for t in range(4):
                            for f in range(FC):
                                ins = pe.matmul(PE[c % 2][:, t * P:(t + 1) * P], MID[c % 2][:, f, t * P:(t + 1) * P],
                                                W2[i][:, f, :], start=(f == 0), stop=(f == FC - 1))
                        ins.then_inc(s_y, 1)


_INS = ['hidden_states', 'Wq', 'bq', 'Wk', 'bk', 'Wv', 'bv']
_FFN = ['ln1_g', 'ln1_b', 'ln2_g', 'ln2_b', 'wq', 'bq', 'wk', 'bk', 'wv', 'bv', 'wo', 'bo', 'gate_w', 'gate_b',
        'w1', 'b1', 'w2', 'b2']
_NAMES = ['L0_attn_' + n for n in _INS] + ['L0_ffn_' + n for n in _FFN]


def kernel(**inputs):
    import numpy as _np
    import concourse.bacc as _bacc
    from concourse import mybir as _mybir
    from concourse.bass_utils import run_bass_kernel_spmd as _run

    nc = _bacc.Bacc("TRN2", target_bir_lowering=False, num_devices=1)
    arrays, args = {}, []
    for name in _NAMES:
        a = _np.ascontiguousarray(inputs[name])
        arrays[f"in_{name}_dram"] = a
        args.append(nc.dram_tensor(f"in_{name}_dram", a.shape, _mybir.dt.from_np(a.dtype), kind="ExternalInput").ap())
    args.append(nc.dram_tensor("out_0_dram", (B, SEQ, HS), F32, kind="ExternalOutput").ap())
    build(nc, *args)
    r = _run(nc, [arrays], core_ids=[0])
    return r.results[0]["out_0_dram"]
```

```python
from contextlib import ExitStack

import numpy as np

import concourse.bass as bass
from concourse import mybir

ALU = mybir.AluOpType
ACT = mybir.ActivationFunctionType
AX_X = mybir.AxisListType.X
F32 = mybir.dt.float32
BF16 = mybir.dt.bfloat16

P = 128
B, SEQ, HS = 2, 1024, 128
H, D = 16, 8
BLK = 64
TT = SEQ // P
G = B * TT
E, F = 8, 512
FC = F // P
PAIRS = H // 2
UNITS = B * PAIRS
SLOTS = G + E
UB = 4
SLOT = 64
MROW = 6 * D
SCALE = float(np.float32(1.0 / np.sqrt(D)))
EPS = 1e-5
HI, MID, LO = (0, 0), (3, 1), (5, 2)
AGAIN = ((0, 1, 0), (0, 2, 0), (0, 4, 3), (1, 3, 0), (1, 5, 0), (1, 4, 1))


def block_col(i):
    return BLK * {0: 0, SEQ // BLK - 1: 1, 1: SEQ // BLK - 1}.get(i, i)


def mm(bank, rows, col, left, right):
    return dict(bank=bank, rows=rows, col=col, left=left, right=right)


ALL, LOW, UPP = (0, P), (0, BLK), (BLK, P)


class Layer:
    pass


def full_layer():
    L = Layer()
    L.slots = 4 * TT
    L.max_steps = [
        dict(h=h, mms=[mm(k, ALL, 0, (t * P, P), (k * 512, 512)) for k in range(2)],
             view=("flat", 1024), out=(h * TT + t, 1, 1))
        for h in range(2) for t in range(TT)]
    L.max_slot = [2 * m for m in range(2 * TT)]
    L.exp_tiles = [
        dict(n=512, mms=[(h, mm(0, ALL, 0, (kt * P, P), (half * 512, 512)))])
        for kt in range(TT) for h in range(2) for half in range(2)]
    L.ring = 8
    L.av_groups = [
        dict(last=4 * kt + 3,
             mms=[(h, half, 4 * kt + 2 * h + half, (0, 512), "full", kt, 0)
                  for h in range(2) for half in range(2)])
        for kt in range(TT)]
    L.av_slot = [4 * g + 5 for g in range(TT)]
    L.kinds = ["full"]
    L.at = dict(MT=2, OT=9, K=14, Q=7, V=16)
    L.lead, L.cut = 12, 14
    L.parts = [(2, 0, -44), (2, 1, -42), (3, 0, -40), (2, 2, -38), (2, 3, -34), (3, 1, -28), (3, 2, -24), (3, 3, -12)]
    return L


def block_layer():
    L = Layer()
    L.slots = 13
    L.max_steps = []
    for h in range(2):
        L.max_steps.append(dict(h=h, mms=[mm(k, ALL, 0, (0, P), (k * 512, 512)) for k in range(2)],
                                view=("flat", 1024), out=(h * TT, 1, 1)))
        for j0 in (1, 3, 5):
            mms = []
            for k in range(2):
                j = j0 + k
                mms += [mm(k, ALL, 0, (j * P, P), (0, P)),
                        mm(k, ALL, P, (j * P, P), (j * P, P)),
                        mm(k, LOW, 2 * P, (j * P, BLK), (block_col(2 * j - 1), BLK)),
                        mm(k, UPP, 2 * P, (j * P + BLK, BLK), (block_col(2 * j + 2), BLK))]
            L.max_steps.append(dict(h=h, mms=mms, view=("banks", 320), out=(h * TT + j0, 2, 1)))
    t7 = (TT - 1) * P
    mms = []
    for h in range(2):
        mms += [(h, mm(h, ALL, 0, (t7, P), (0, P))),
                (h, mm(h, LOW, P, (t7, BLK), (block_col(13), P))),
                (h, mm(h, UPP, P, (t7 + BLK, BLK), (block_col(1), BLK))),
                (h, mm(h, UPP, P + BLK, (t7 + BLK, BLK), (block_col(2), BLK)))]
    L.max_steps.append(dict(h=None, mms=mms, view=("banks", 256), out=(TT - 1, 2, TT)))
    L.max_slot = [0, 2, 3, 4, 6, 7, 9, 10, 12]

    def single(j, col):
        return [mm(0, LOW, col, (block_col(2 * j + 2), BLK), (j * P + BLK, BLK)),
                mm(0, UPP, col, (block_col(2 * j - 1), BLK), (j * P, BLK))]

    def single_v(h, e, j, col):
        q0, q1 = j * P, j * P + BLK
        return [(h, q0 // 512, e, (col, BLK), "upp", block_col(2 * j - 1) // P, q0 % 512),
                (h, q1 // 512, e, (col, BLK), "low", block_col(2 * j + 2) // P, q1 % 512)]

    t1, t6 = block_col(2) // P, block_col(13) // P
    tiles, groups = [], []
    for kind in range(6):
        group = dict(last=2 * kind + 1, mms=[])
        per_head = []
        for h in range(2):
            e, v = 2 * kind + h, []
            if kind < 2:
                ts = range(4 * kind, 4 * kind + 4)
                mms = [mm(0, ALL, i * P, (t * P, P), (0, P)) for i, t in enumerate(ts)]
                v = [(h, 0, e, (i * P, P), "full", t, 0) for i, t in enumerate(ts)]
                n = 512
            elif kind == 2:
                mms = [mm(0, ALL, 0, (0, P), (P, 512))]
                v = [(h, 0, e, (0, 384), "full", 0, P), (h, 1, e, (384, P), "full", 0, 0)]
                n = 512
            elif kind == 3:
                mms = [mm(0, ALL, 0, (0, P), (640, 384)),
                       mm(0, LOW, 384, (block_col(14), BLK), (t7, BLK)),
                       mm(0, UPP, 384, (block_col(13), BLK), (t7, BLK)),
                       mm(0, LOW, 448, (block_col(2), BLK), (t7 + BLK, BLK)),
                       mm(0, UPP, 448, (block_col(1), BLK), (t7 + BLK, BLK))]
                v = [(h, 1, e, (0, 384), "full", 0, P),
                     (h, 1, e, (384, BLK), "low", TT - 1, 384), (h, 1, e, (384, BLK), "upp", t6, 384),
                     (h, 1, e, (448, BLK), "low", t1, 448), (h, 1, e, (448, BLK), "upp", TT - 1, 448)]
                n = 512
            elif kind == 4:
                mms = [mm(0, ALL, (j - 1) * P, (j * P, P), (j * P, P)) for j in range(1, 5)]
                v = [(h, j // 4, e, ((j - 1) * P, P), "full", j, j % 4 * P) for j in range(1, 5)]
                n = 512
            else:
                mms = [mm(0, ALL, (j - 5) * P, (j * P, P), (j * P, P)) for j in (5, 6)]
                v = [(h, 1, e, ((j - 5) * P, P), "full", j, j % 4 * P) for j in (5, 6)]
                for j in range(1, 5):
                    mms += single(j, 256 + (j - 1) * BLK)
                    v += single_v(h, e, j, 256 + (j - 1) * BLK)
                n = 512
            tiles.append(dict(n=n, mms=[(h, m) for m in mms]))
            per_head.append(v)
        for a, b in zip(*per_head):
            group["mms"] += [a, b]
        groups.append(group)
    mms, per_head = [], []
    for h in range(2):
        v = []
        for j in (5, 6):
            col = h * P + (j - 5) * BLK
            mms += [(h, m) for m in single(j, col)]
            v += single_v(h, 12, j, col)
        per_head.append(v)
    tiles.append(dict(n=2 * P, mms=mms))
    groups.append(dict(last=12, mms=[x for pair in zip(*per_head) for x in pair]))
    L.exp_tiles, L.av_groups = tiles, groups
    L.ring = len(tiles)
    L.av_slot = [2 * g + 3 for g in range(6)] + [14]
    L.kinds = ["full", "low", "upp"]
    L.at = dict(MT=3, OT=5, K=7, Q=4, V=8)
    L.lead, L.cut = 10, 20
    L.parts = [(2, 0, -22), (2, 1, -21), (3, 0, -20), (2, 2, -18), (2, 3, -16), (3, 1, -12), (3, 2, -9), (3, 3, -3)]
    return L


def mark_ends(L):
    flat = [(g, i, m[:2]) for g, gr in enumerate(L.av_groups) for i, m in enumerate(gr["mms"])]
    first, last = {}, {}
    for g, i, key in flat:
        first.setdefault(key, (g, i))
        last[key] = (g, i)
    for g, gr in enumerate(L.av_groups):
        gr["mms"] = [m + (first[m[:2]] == (g, i), last[m[:2]] == (g, i)) for i, m in enumerate(gr["mms"])]
    return L


def plan(L):
    S, acts = L.slots, []
    for u in range(UNITS):
        acts += [(u * S + e, 0, "EXP", u, e) for e in range(len(L.exp_tiles))]
        t0 = (u - 1) * S - L.lead
        acts += [(t0 + s, 1, "MAX", u, m) for m, s in enumerate(L.max_slot)]
        acts += [(u * S + s, 2, "AV", u, g) for g, s in enumerate(L.av_slot)]
        acts += [(u * S + L.av_slot[-1], 3, "OE", u, 0)]
        acts += [(t0 + S + L.at["MT"], 4, "MT", u, 0), ((u + 1) * S + L.at["OT"], 5, "OT", u, 0)]
        acts += [((u - 1) * S + L.at["V"], 8, "V", u, 0)]
        acts += [(t0 - L.at["K"], 6, "K", u, 0), (t0 - L.at["Q"], 7, "Q", u, 0)]
    acts += [(t, 9, "PART", q, k) for q, k, t in L.parts]
    acts.sort()
    shared, before = {}, None
    for _, _, kind, u, _ in acts:
        if kind in ("K", "Q", "MT", "OT"):
            shared[kind, u] = before
            before = (kind, u)
    rounds = (UNITS - UB) // UB
    lo, hi = L.cut, L.cut + UB * S
    body = [a for a in acts if lo <= a[0] < hi]
    for r in range(1, rounds):
        again = [(t + r * UB * S, p, k, u + r * UB, x) for t, p, k, u, x in body]
        assert again == [a for a in acts if lo + r * UB * S <= a[0] < hi + r * UB * S]
    head = [a for a in acts if a[0] < lo]
    tail = [a for a in acts if a[0] >= lo + rounds * UB * S]
    return [[a[2:] for a in part] for part in (head, body, tail)], rounds, shared


def build(nc, x, Wq, bq, Wk, bk, Wv, bv, ln1_g, ln1_b, ln2_g, ln2_b, fwq, fbq, fwk, fbk, fwv, fbv, fwo, fbo,
          gate_w, gate_b, w1, b1, w2, b2, out):
    LAYERS = [mark_ends(block_layer()), mark_ends(full_layer())]
    PLANS = [plan(L) for L in LAYERS]
    with ExitStack() as ctx:
        def sb(name, shape, dt=F32):
            return ctx.enter_context(nc.sbuf_tensor(name, shape, dt))

        def pb(name, shape, dt=F32):
            return ctx.enter_context(nc.psum_tensor(name, shape, dt))

        def sem(name):
            return ctx.enter_context(nc.semaphore(name))

        X = sb("X", [P, G, HS])
        X1 = sb("X1", [P, G, HS])
        CTX = sb("CTX", [P, TT, B, H * D])
        XT = sb("XT", [P, G * P])
        QKV = sb("QKV", [P, G, 2 * HS])
        VST = sb("VST", [P, TT, B, H * D])
        QK = sb("QK", [P, 2, TT, B, H, SLOT], BF16)
        WQKV = sb("WQKV", [P, 3 * HS])
        WF = sb("WF", [P, 3 * HS])
        BIAS = sb("BIAS", [P, 2, 3 * HS])
        WO = sb("WO", [P, HS])
        GW = sb("GW", [P, E])
        ROWS = sb("ROWS", [P, 5, HS])
        GB = sb("GB", [P, E])
        B1R = sb("B1R", [E * FC, P])
        B1T = sb("B1T", [P, E * FC])
        IDF = sb("IDF", [P, P])
        IDB = sb("IDB", [P, P], BF16)
        QT = [sb(f"QT{i}", [P, SEQ], BF16) for i in range(UB)]
        KT = [sb(f"KT{i}", [P, 2, SEQ], BF16) for i in range(UB)]
        VB = [sb(f"VB{i}", [P, 3, TT, 2, 32]) for i in range(2)]
        PR = sb("PR", [P, 13, 512])
        NM = [sb(f"NM{i}", [P, 2 * TT]) for i in range(2)]
        NR = [sb(f"NR{i}", [P, 2 * TT]) for i in range(2)]
        MS = [sb(f"MS{i}", [P, 2, 3, TT], BF16) for i in range(2)]
        MT = [sb(f"MT{i}", [6 * TT, P], BF16) for i in range(2)]
        OS = sb("OS", [P, 512])
        WRAW = OS[:, 0:3 * HS].rearrange("p (i c) -> p i c", i=3)
        RS = sb("RS", [P, 2 * TT])
        ST = sb("ST", [P, G, 6])
        MV = sb("MV", [P, G, 2])
        VE = sb("VE", [P, G])
        SD = sb("SD", [P, G])
        RD = sb("RD", [P, G])
        LG = sb("LG", [P, G, E])
        LE = sb("LE", [P, G, E])
        LM = sb("LM", [P, G])
        OH = sb("OH", [P, G, E])
        RANK = sb("RANK", [P, E])
        PREF = sb("PREF", [P, G, E])
        CUM = [sb(f"CUM{i}", [P, G, E]) for i in range(2)]
        TOT = sb("TOT", [P, G, E])
        TL = sb("TL", [P, E])
        EN = [sb(f"EN{i}", [P, E]) for i in range(2)]
        S128 = sb("S128", [P, E])
        POSF = sb("POSF", [P, G])
        POS = sb("POS", [P, G], mybir.dt.uint32)
        EJF = sb("EJF", [P, SLOTS])
        EJ = sb("EJ", [P, SLOTS], mybir.dt.int32)
        CMP = sb("CMP", [P, SLOTS, E])
        JC = sb("JC", [P, SLOTS])
        KC = sb("KC", [P, G])
        TRI = sb("TRI", [P, P])
        ONES = sb("ONES", [P, P])
        free = QK[:].rearrange("p w t b h s -> p (w t b h s)").bitcast(F32)
        W1A = free[:, 0:E * F].rearrange("p (e f) -> p e f", e=E)
        W2A = free[:, E * F:2 * E * F].rearrange("p (e n) -> p e n", n=HS)
        B2A = free[:, 2 * E * F:2 * E * F + E * HS].rearrange("p (e n) -> p e n", n=HS)
        o = 2 * E * F + E * HS
        XSB = free[:, o:o + SLOTS * HS].rearrange("p (s n) -> p s n", n=HS)
        YSB = free[:, o + SLOTS * HS:o + 2 * SLOTS * HS].rearrange("p (s n) -> p s n", n=HS)
        H1 = [PR[:, i, :] for i in range(3)]
        HT = [PR[:, 3 + i, :] for i in range(3)]
        XST = PR[:, 6:6 + SLOTS // 4, :].rearrange("p a b -> p (a b)")
        XC = PR[:, 12, 0:3 * P]
        MOE = CTX[:].rearrange("p t b c -> p (t b) c")
        ZERO = VST[:].rearrange("p t b c -> p (t b) c")
        XS = nc.dram_tensor("sorted_rows", (SLOTS * P, HS), F32).ap()
        YS = nc.dram_tensor("sorted_results", (SLOTS * P, HS), F32).ap()
        HN2 = QKV[:].rearrange("p g c -> p (g c)")[:, 0:G * HS].rearrange("p (g c) -> p g c", g=G)

        PM = [pb(f"PM{i}", [P, 1024]) for i in range(2)]
        PE = [pb(f"PE{i}", [P, 512]) for i in range(2)]
        PO = pb("PO", [P, 512])
        PX = pb("PX", [P, 512])
        PXB = PX[:].bitcast(BF16)
        YB = [PE[0][:, 0:HS], PE[1][:, 0:HS], PM[0][:, 0:HS]]
        TB = [PX, PO, PM[1][:, 512:1024]]
        PMR = [PM[i // 2][:, 512 * (i % 2):512 * (i % 2) + 512] for i in range(4)]

        s_x = sem("s_x"); s_w = sem("s_w"); s_small = sem("s_small"); s_out = sem("s_out")
        s_ident = sem("s_ident"); s_init = sem("s_init"); s_const = sem("s_const"); s_rank = sem("s_rank")
        s_wt = sem("s_wt"); s_wready = sem("s_wready"); s_bscaled = sem("s_bscaled")
        s_src = sem("s_src")
        s_xt = sem("s_xt"); s_xte = sem("s_xte")
        s_proj = sem("s_proj"); s_proje = sem("s_proje")
        s_part = sem("s_part"); s_rem = [sem(f"s_rem{b}") for b in range(B)]
        s_parts = [sem(f"s_parts{b}") for b in range(B)]
        s_trans = sem("s_trans"); s_qk = sem("s_qk"); s_k1 = sem("s_k1")
        s_maxmm = sem("s_maxmm"); s_max = sem("s_max"); s_split = sem("s_split")
        s_mt = sem("s_mt"); s_mte = sem("s_mte"); s_mrow = sem("s_mrow")
        s_sc = sem("s_sc"); s_exp = sem("s_exp"); s_v = sem("s_v")
        s_av = sem("s_av"); s_oe = sem("s_oe"); s_ot = sem("s_ot"); s_rs = sem("s_rs"); s_ctx = sem("s_ctx")
        s_dve = sem("s_dve")
        s_var = sem("s_var"); s_std = sem("s_std")
        s_wo = sem("s_wo"); s_gate = sem("s_gate"); s_oh = sem("s_oh")
        s_count = sem("s_count"); s_pos = sem("s_pos"); s_zero = sem("s_zero"); s_zeroed = sem("s_zeroed")
        s_tri = sem("s_tri"); s_jc = sem("s_jc"); s_we = sem("s_we"); s_scat = sem("s_scat"); s_xs = [sem(f"s_xs{i}") for i in range(SLOTS // 8)]
        s_xc = sem("s_xc"); s_h = sem("s_h"); s_he = sem("s_he"); s_ht = sem("s_ht"); s_hte = sem("s_hte")
        s_y = sem("s_y"); s_ye = sem("s_ye"); s_ys = sem("s_ys"); s_back = sem("s_back")
        s_fin = sem("s_fin")

        NCONST = UB + 3 * TT + E
        NX = [len(L.exp_tiles) for L in LAYERS]
        NMX = [len(L.max_steps) for L in LAYERS]
        NAV = [len(L.av_groups) for L in LAYERS]
        BX = [0, UNITS * NX[0]]
        BM = [0, UNITS * NMX[0]]
        BA = [0, UNITS * NAV[0]]
        BU = [0, UNITS]

        def wait(eng, s, value):
            if not (isinstance(value, int) and value <= 0):
                eng.wait_ge(s, value)

        def run(eng, li, do):
            (head, body, tail), rounds, _ = PLANS[li]
            for kind, u, k in head:
                do(kind, u, u, k)
            with eng.Fori(0, rounds) as r:
                for kind, u, k in body:
                    do(kind, u, r * UB + u, k)
            for kind, u, k in tail:
                do(kind, u + 0, u, k)

        def part(w, t0, b, place):
            return QK[:, w, t0:t0 + 4, b, :, place * D:(place + 1) * D]

        def rest(q, w):
            return QKV[:, 4 * q:4 * q + 4, w * HS:(w + 1) * HS].rearrange("p t (h d) -> p t h d", d=D)

        def part_count(li, q, k):
            order = [(0, 0), (1, 0), (0, 2), (1, 2)] + [(a, c) for a, c, _ in sorted(LAYERS[li].parts, key=lambda z: z[2])
                                                      if c in (0, 2)]
            return 16 * li + 2 * order.index((q, k)) + 2

        block = ctx.enter_context(nc.Block())

        @block.sync
        def _(sp):
            for b in range(B):
                xb = x[b]
                g = b * TT
                sp.dma_start(X[:, g + 1:g + 7, :], xb[P:7 * P, :].rearrange("(j p) c -> p j c", p=P)).then_inc(s_x, 16)
                for t, half, blk in ((0, 0, 0), (0, 1, 15), (7, 0, 14), (7, 1, 1)):
                    sp.dma_start(X[half * BLK:(half + 1) * BLK, g + t, :],
                                 xb[blk * BLK:(blk + 1) * BLK, :]).then_inc(s_x, 16)
            for i, w in enumerate((Wq, Wk, Wv)):
                sp.dma_start(WRAW[:, i, :], w[:, :]).then_inc(s_w, 16)
            for i, v in enumerate((bq, bk, bv, fbq, fbk, fbv)):
                sp.dma_start(BIAS[:, i // 3, (i % 3) * HS:(i % 3 + 1) * HS], v.partition_broadcast(P)).then_inc(s_w, 16)
            for i, w in enumerate((fwq, fwk, fwv)):
                sp.dma_start(WF[:, i * HS:(i + 1) * HS], w[:, :]).then_inc(s_small, 16)
            sp.dma_start(WO[:], fwo[:, :]).then_inc(s_small, 16)
            sp.dma_start(GW[:], gate_w[:, :]).then_inc(s_small, 16)
            sp.dma_start(GB[:], gate_b.partition_broadcast(P)).then_inc(s_small, 16)
            for i, v in enumerate((ln1_g, ln1_b, ln2_g, ln2_b, fbo)):
                sp.dma_start(ROWS[:, i, :], v.partition_broadcast(P)).then_inc(s_small, 16)
            sp.dma_start(B1R[:], b1.rearrange("e (c f) -> (e c) f", f=P)).then_inc(s_small, 16)
            sp.wait_ge(s_zero, 1)
            for i in range(SLOTS // 8):
                sp.dma_start(XS[i * 8 * P:(i + 1) * 8 * P, :].rearrange("(s p) n -> p s n", p=P),
                             ZERO[:, 0:8, :]).then_inc(s_zeroed, 16)

            for li in range(2):
                def do(kind, u0, u, k, li=li):
                    if kind == "MT":
                        sp.wait_ge(s_mte, BU[li] + u + 1)
                        for h in range(2):
                            row = h * SLOT + MROW
                            sp.dma_start(QT[u0 % UB][row:row + 3, :].rearrange("s (t q) -> s t q", t=TT),
                                         MT[u0 % 2][h * 3 * TT:(h + 1) * 3 * TT, :]).then_inc(s_mrow, 16)
                run(sp, li, do)

            sp.wait_ge(s_trans, 4 * UNITS)
            sp.dma_start(W1A, w1.rearrange("e h f -> h e f")).then_inc(s_we, 16)
            sp.dma_start(W2A, w2.rearrange("e (c f) n -> f (e c) n", f=P)).then_inc(s_we, 16)
            sp.dma_start(B2A, b2.rearrange("e n -> (e n)").partition_broadcast(P).rearrange("p (e n) -> p e n", n=HS)
                         ).then_inc(s_we, 16)
            sp.wait_ge(s_scat, 16 * G)
            for i in range(SLOTS // 8):
                sp.dma_start(XSB[:, 8 * i:8 * i + 8, :],
                             XS[i * 8 * P:(i + 1) * 8 * P, :].rearrange("(s p) n -> p s n", p=P)).then_inc(s_xs[i], 16)
            for i in range(SLOTS // 3):
                sp.wait_ge(s_ye, 3 * (i + 1) + 3)
                sp.dma_start(YS[i * 3 * P:(i + 1) * 3 * P, :].rearrange("(s p) n -> p s n", p=P),
                             YSB[:, 3 * i:3 * i + 3, :]).then_inc(s_ys, 16)

            for b in range(B):
                g = b * TT
                sp.wait_ge(s_fin, (b + 1) * TT)
                ob = out[b]
                sp.dma_start(ob[P:7 * P, :].rearrange("(j p) c -> p j c", p=P), X1[:, g + 1:g + 7, :]).then_inc(s_out, 16)
                for t, half, blk in ((0, 0, 0), (0, 1, 15), (7, 0, 14), (7, 1, 1)):
                    sp.dma_start(ob[blk * BLK:(blk + 1) * BLK, :],
                                 X1[half * BLK:(half + 1) * BLK, g + t, :]).then_inc(s_out, 16)
            sp.wait_ge(s_out, 16 * 5 * B)

        @block.gpsimd
        def _(pool):
            nc.gpsimd.memset(IDF[:], 0.0).then_inc(s_rank, 1)
            nc.gpsimd.memset(IDB[:], 0.0).then_inc(s_rank, 1)
            pool.wait_ge(s_rank, 2)
            for t in (IDF, IDB):
                nc.gpsimd.affine_select(out=t[:], in_=t[:], compare_op=ALU.not_equal, fill=1.0, base=0,
                                        pattern=[[-1, P]], channel_multiplier=1).then_inc(s_ident, 1)
            nc.gpsimd.memset(ONES[:], 1.0).then_inc(s_tri, 1)
            nc.gpsimd.memset(TRI[:], 1.0).then_inc(s_tri, 1)
            pool.wait_ge(s_tri, 2)
            nc.gpsimd.affine_select(out=TRI[:], in_=TRI[:], compare_op=ALU.is_gt, fill=0.0, base=0,
                                    pattern=[[1, P]], channel_multiplier=-1).then_inc(s_tri, 1)
            for j in range(SLOTS):
                nc.gpsimd.memset(JC[:, j:j + 1], float(j)).then_inc(s_jc, 1)
            pool.wait_ge(s_jc, SLOTS)
            nc.gpsimd.tensor_scalar(KC[:], JC[:, 0:G], float(P), None, ALU.mult).then_inc(s_jc, 1)
            pool.wait_ge(s_ident, 2)
            n = 0
            for i in range(2):
                for kind, rows in enumerate((ALL, ALL, LOW, UPP)):
                    if kind == 0:
                        nc.gpsimd.memset(VB[i][:], 0.0).then_inc(s_init, 1)
                    else:
                        nc.gpsimd.memset(VB[i][rows[0]:rows[1], kind - 1, :, :, D:D + 1], 1.0).then_inc(s_init, 1)
                    n += 1
                    pool.wait_ge(s_init, n)

            for li, L in enumerate(LAYERS):
                def do(kind, u0, u, k, li=li, L=L):
                    if kind == "PART" and k == 1:
                        pool.wait_ge(s_proje, 2 * (G * li + 4 * u + 4))
                        pool.wait_ge(s_part, part_count(li, u, 0))
                        for w in range(2):
                            nc.gpsimd.tensor_tensor(rest(u, w), rest(u, w), part(w, 4 * (u - 2), 1, HI[w]),
                                                    ALU.subtract).then_inc(s_rem[1], 1)
                    if kind == "V":
                        if u0 == 0 and k == 0 and isinstance(u, int):
                            pool.wait_ge(s_proje, 2 * G * (li + 1))
                        wait(pool, s_av, (u - 1) * NAV[li] + BA[li] if not isinstance(u, int) or u >= 2
                             else BA[li])
                        src = VST[:].rearrange("p t b c -> p t (b c)")[:, :, bass.ds(u * 2 * D, 2 * D)] \
                            .rearrange("p t (h d) -> p t h d", h=2)
                        pool.nop(nofuse=True)
                        for i, kd in enumerate(L.kinds):
                            lo, hi = {"full": ALL, "low": LOW, "upp": UPP}[kd]
                            nc.gpsimd.tensor_copy(VB[u0 % 2][lo:hi, i, :, :, 0:D], src[lo:hi]).then_inc(s_v, 1)
                            pool.wait_ge(s_v, (3 * UNITS if li else 0) + u * len(L.kinds) + (i + 1))
                            pool.nop(nofuse=True)
                    if kind == "MT":
                        a, r, m = NM[u0 % 2], NR[u0 % 2], MS[u0 % 2]
                        a3 = a[:].rearrange("p (h t) -> p h t", h=2)
                        r3 = r[:].rearrange("p (h t) -> p h t", h=2)
                        c = BU[li] * 4 + u * 4
                        pool.wait_ge(s_max, BM[li] + (u + 1) * NMX[li])
                        wait(pool, s_mt, BU[li] + u - 1)
                        pool.nop(nofuse=True)
                        nc.gpsimd.tensor_copy(m[:, :, 0, :], a3).then_inc(s_split, 1)
                        pool.wait_ge(s_split, c + 1)
                        nc.gpsimd.tensor_tensor(r3, a3, m[:, :, 0, :], ALU.subtract).then_inc(s_split, 1)
                        pool.wait_ge(s_split, c + 2)
                        pool.nop(nofuse=True)
                        nc.gpsimd.tensor_copy(m[:, :, 1, :], r3).then_inc(s_split, 1)
                        pool.wait_ge(s_split, c + 3)
                        nc.gpsimd.tensor_tensor(m[:, :, 2, :], r3, m[:, :, 1, :], ALU.subtract).then_inc(s_split, 1)
                run(pool, li, do)

            pool.wait_ge(s_pos, 1)
            pool.wait_ge(s_zeroed, 16 * (SLOTS // 8))
            for g in range(G):
                pool.indirect_dma_start(out=XS, out_offset=bass.IndirectOffsetOnAxis(ap=POS[:, g:g + 1], axis=0),
                                        in_=HN2[:, g, :], in_offset=None).then_inc(s_scat, 16)
            pool.wait_ge(s_xte, 16 + SLOTS // 4)
            with pool.Fori(0, SLOTS // 3) as r:
                for i in range(3):
                    n = r * 3 + i
                    pool.wait_ge(s_h, n + 1)
                    pool.nop(nofuse=True)
                    nc.gpsimd.tensor_copy(XC[:, i * P:(i + 1) * P], XST[:, bass.ds(n * P, P)]).then_inc(s_xc, 1)
            pool.wait_ge(s_ys, 16 * (SLOTS // 3))
            for g in range(G):
                pool.indirect_dma_start(out=MOE[:, g, :], out_offset=None, in_=YS,
                                        in_offset=bass.IndirectOffsetOnAxis(ap=POS[:, g:g + 1], axis=0)
                                        ).then_inc(s_back, 16)

        @block.scalar
        def _(act):
            act.wait_ge(s_wt, 3)
            nc.scalar.mul(WQKV[:, 0:HS], PX[:, 0:HS], SCALE).then_inc(s_wready, 1)
            nc.scalar.copy(WQKV[:, HS:3 * HS], PX[:, HS:3 * HS]).then_inc(s_wready, 1)
            act.wait_ge(s_w, 16 * 9)
            for i in range(2):
                nc.scalar.mul(BIAS[:, i, 0:HS], BIAS[:, i, 0:HS], SCALE).then_inc(s_bscaled, 1)

            def parts(li, q, k):
                b, t0 = divmod(4 * q, TT)
                if k == 0:
                    act.wait_ge(s_proje, 2 * (G * li + 4 * q + 4))
                else:
                    act.wait_ge(s_rem[b], 4 * li + 2 * (q % 2) + 2)
                for w in range(2):
                    nc.scalar.copy(part(w, t0, b, (HI, MID)[k // 2][w]), rest(q, w)).then_inc(s_part, 1)

            def project(li):
                for q in range(G // 4):
                    act.wait_ge(s_xt, 4 * li + q + 1)
                    nc.scalar.copy(XT[:, q * 512:(q + 1) * 512], PE[q % 2][:]).then_inc(s_xte, 1)
                for q in range(2):
                    parts(li, q, 0)
                for q in range(2):
                    parts(li, q, 2)

            for li, L in enumerate(LAYERS):
                if li == 1:
                    for n in range(2):
                        act.wait_ge(s_var, n + 1)
                        nc.scalar.activation(SD[:], VE[:], ACT.Sqrt).then_inc(s_std, 1)
                    act.wait_ge(s_small, 16 * 12)
                    nc.scalar.mul(WF[:, 0:HS], WF[:, 0:HS], SCALE).then_inc(s_wready, 1)
                project(li)

                def do(kind, u0, u, k, li=li, L=L):
                    if kind == "K":
                        wait(act, s_sc, BX[li] + (u - UB + 1) * NX[li] if not isinstance(u, int) or u >= UB
                             else BX[li])
                        act.wait_ge(s_trans, 2 * BU[li] + 2 * u + 1)
                        nc.scalar.copy(KT[u0 % UB][0:SLOT, 0, :], PXB[0:SLOT, :]).then_inc(s_qk, 1)
                    if kind == "PART" and k in (0, 2):
                        parts(li, u, k)
                    if kind == "Q":
                        act.wait_ge(s_trans, 2 * BU[li] + 2 * u + 2)
                        nc.scalar.copy(QT[u0 % UB][:], PXB).then_inc(s_qk, 1)
                    if kind == "EXP":
                        n = L.exp_tiles[k]["n"]
                        count = BX[li] + u * NX[li] + k
                        act.wait_ge(s_sc, count + 1)
                        e = k - L.ring
                        du = 0
                        while e < 0:
                            e += NX[li]
                            du -= 1
                        g = [i for i, gr in enumerate(L.av_groups) if gr["last"] >= e][0]
                        if li == 1 and isinstance(u, int) and u == 0 and k == 0:
                            act.wait_ge(s_av, BA[1])
                        if not isinstance(u, int) or u + du >= 0:
                            act.wait_ge(s_av, BA[li] + (u + du) * NAV[li] + g + 1)
                        nc.scalar.activation(PR[:, k % L.ring, 0:n], PE[(u0 * NX[li] + k) % 2][:, 0:n],
                                             ACT.Exp).then_inc(s_exp, 1)
                run(act, li, do)

            for n in range(2):
                for q in range(G // 4):
                    act.wait_ge(s_xt, 8 + 4 * n + q + 1)
                    nc.scalar.copy(XT[:, q * 512:(q + 1) * 512], PE[q % 2][:]).then_inc(s_xte, 1)
                if n == 0:
                    act.wait_ge(s_wt, 4)
                    nc.scalar.copy(B1T[:], PX[:, 0:E * FC]).then_inc(s_wready, 1)
                    act.wait_ge(s_var, 3)
                    nc.scalar.activation(SD[:], VE[:], ACT.Sqrt).then_inc(s_std, 1)
            for q in range(SLOTS // 4):
                act.wait_ge(s_xt, 16 + q + 1)
                nc.scalar.copy(XST[:, q * 512:(q + 1) * 512], PE[q % 2][:]).then_inc(s_xte, 1)
            act.nop(nofuse=True).then_inc(s_he, 3)
            with act.Fori(0, SLOTS // 3) as r:
                for i in range(3):
                    n = r * 3 + i
                    act.wait_ge(s_h, n + 4)
                    act.wait_ge(s_ht, n + 1)
                    nc.scalar.copy(H1[i], PMR[i]).then_inc(s_he, 1)
            act.wait_ge(s_var, 4)
            nc.scalar.activation(SD[:], VE[:], ACT.Sqrt).then_inc(s_std, 1)

        @block.vector
        def _(dve):
            chain = [0]

            def link(ins):
                chain[0] += 1
                ins.then_inc(s_dve, 1)
                dve.wait_ge(s_dve, chain[0])

            def step(ins):
                chain[0] += 1
                ins.then_inc(s_dve, 1)

            nc.vector.memset(ZERO, 0.0).then_inc(s_zero, 1)
            for i in range(UB):
                nc.vector.memset(KT[i][:], 0.0).then_inc(s_const, 1)
            for w in range(2):
                for t in range(TT):
                    nc.vector.memset(QK[:, w, t, :, :, MROW:SLOT], 0.0).then_inc(s_const, 1)
            dve.wait_ge(s_const, UB + 2 * TT)
            for t in range(TT):
                nc.vector.memset(QK[:, 1, t, :, :, MROW:MROW + 3], 1.0).then_inc(s_const, 1)
            for e in range(E):
                nc.vector.memset(RANK[:, e:e + 1], float(E - e)).then_inc(s_const, 1)
            dve.wait_ge(s_const, NCONST)

            def project(li):
                bias = BIAS[:, li, :]
                dve.wait_ge(s_bscaled, 2)
                for g in range(G):
                    b, t = divmod(g, TT)
                    ps = PMR[g % 4]
                    dve.wait_ge(s_proj, G * li + g + 1)
                    if g == 0:
                        if li == 1:
                            dve.wait_ge(s_v, 3 * UNITS)
                        else:
                            dve.wait_ge(s_zeroed, 16 * (SLOTS // 8))
                    nc.vector.tensor_tensor(QKV[:, g, :], ps[:, 0:2 * HS], bias[:, 0:2 * HS], ALU.add).then_inc(s_proje, 1)
                    nc.vector.tensor_tensor(VST[:, t, b, :], ps[:, 2 * HS:3 * HS], bias[:, 2 * HS:3 * HS],
                                            ALU.add).then_inc(s_proje, 1)
                for q in range(2):
                    dve.wait_ge(s_proje, 2 * (G * li + 4 * q + 4))
                    dve.wait_ge(s_part, part_count(li, q, 0))
                    for w in range(2):
                        nc.vector.tensor_tensor(rest(q, w), rest(q, w), part(w, 4 * q, 0, HI[w]),
                                                ALU.subtract).then_inc(s_rem[0], 1)
                for q in range(2):
                    dve.wait_ge(s_part, part_count(li, q, 2))
                    for w in range(2):
                        nc.vector.tensor_tensor(part(w, 4 * q, 0, LO[w]), rest(q, w), part(w, 4 * q, 0, MID[w]),
                                                ALU.subtract).then_inc(s_parts[0], 1)
                    for w, to, of in AGAIN:
                        nc.vector.tensor_copy(part(w, 4 * q, 0, to), part(w, 4 * q, 0, of)).then_inc(s_parts[0], 1)

            def norm(src, dst, n, fin=None):
                for g in range(G):
                    step(nc.vector.bn_stats(ST[:, g, :], src[:, g, :]))
                dve.wait_ge(s_dve, chain[0])
                for g in range(G):
                    step(nc.vector.bn_aggr(MV[:, g, :], ST[:, g, :]))
                dve.wait_ge(s_dve, chain[0])
                nc.vector.tensor_scalar(VE[:], MV[:, :, 1], EPS, None, ALU.add).then_inc(s_var, 1)
                dve.wait_ge(s_std, n)
                link(nc.vector.reciprocal(RD[:], SD[:]))
                for g in range(G):
                    ins = nc.vector.tensor_scalar(dst[:, g, :], src[:, g, :], MV[:, g, 0:1], RD[:, g:g + 1],
                                                  ALU.subtract, ALU.mult)
                    if fin is None:
                        step(ins)
                    else:
                        ins.then_inc(fin, 1)
                if fin is None:
                    dve.wait_ge(s_dve, chain[0])

            def affine(dst, k):
                link(nc.vector.tensor_tensor(dst, dst, ROWS[:, k:k + 1, :].broadcast_to([P, G, HS]), ALU.mult))
                nc.vector.tensor_tensor(dst, dst, ROWS[:, k + 1:k + 2, :].broadcast_to([P, G, HS]),
                                        ALU.add).then_inc(s_src, 1)

            for li, L in enumerate(LAYERS):
                if li == 1:
                    dve.wait_ge(s_x, 16 * 10)
                    dve.wait_ge(s_ctx, 2 * UNITS)
                    xv = X[:].rearrange("p (b t) c -> p t b c", b=B)
                    for b in range(B):
                        link(nc.vector.tensor_tensor(xv[:, :, b, :], xv[:, :, b, :], CTX[:, :, b, :], ALU.add))
                    norm(X, X1, 1)
                    norm(X1, X, 2)
                    dve.wait_ge(s_small, 16 * 12)
                    affine(X[:], 0)
                project(li)

                def do(kind, u0, u, k, li=li, L=L):
                    if kind == "K":
                        wait(dve, s_sc, BX[li] + (u - UB + 1) * NX[li] if not isinstance(u, int) or u >= UB
                             else BX[li])
                        dve.wait_ge(s_trans, 2 * BU[li] + 2 * u + 1)
                        nc.vector.tensor_copy(KT[u0 % UB][SLOT:P, 1, :], PXB[SLOT:P, :]).then_inc(s_k1, 1)
                    if kind == "MAX":
                        st = L.max_steps[k]
                        pm = PM[(u0 * NMX[li] + k) % 2]
                        dve.wait_ge(s_maxmm, BM[li] + u * NMX[li] + k + 1)
                        if k == 0:
                            wait(dve, s_split, 4 * (BU[li] + u - 1))
                        c, n, step_ = st["out"]
                        o = NM[u0 % 2][:, c:c + (n - 1) * step_ + 1:step_]
                        kind_, w = st["view"]
                        if kind_ == "flat":
                            i = pm[:]
                        else:
                            i = pm[:].rearrange("p (k n) -> p k n", k=2)[:, :, 0:w]
                        nc.vector.tensor_reduce(o, i, AX_X, ALU.max, negate=True).then_inc(s_max, 1)
                    if kind == "MT":
                        dve.wait_ge(s_mt, BU[li] + u + 1)
                        wait(dve, s_mrow, 32 * (BU[li] + u - 1))
                        nc.vector.tensor_copy(MT[u0 % 2][:], PXB[0:6 * TT, 0:P]).then_inc(s_mte, 1)
                    if kind == "PART" and k == 3:
                        dve.wait_ge(s_part, part_count(li, u, 2))
                        for w in range(2):
                            nc.vector.tensor_tensor(part(w, 4 * (u - 2), 1, LO[w]), rest(u, w),
                                                    part(w, 4 * (u - 2), 1, MID[w]), ALU.subtract).then_inc(s_parts[1], 1)
                        for w, to, of in AGAIN:
                            nc.vector.tensor_copy(part(w, 4 * (u - 2), 1, to),
                                                  part(w, 4 * (u - 2), 1, of)).then_inc(s_parts[1], 1)
                    if kind == "OE":
                        dve.wait_ge(s_av, BA[li] + (u + 1) * NAV[li])
                        wait(dve, s_ot, BU[li] + u)
                        nc.vector.tensor_copy(OS[:], PO[:]).then_inc(s_oe, 1)
                    if kind == "OT":
                        px = PX[:].rearrange("p (c h a d) -> p c h a d", c=4, h=2, a=2)
                        rs = RS[:].rearrange("p (c h a) -> p c h a", c=4, h=2)
                        dve.wait_ge(s_ot, BU[li] + u + 1)
                        wait(dve, s_ctx, 2 * (BU[li] + u))
                        nc.vector.reciprocal(RS[:], PX[:].rearrange("p (c d) -> p c d", d=32)[:, :, D]).then_inc(s_rs, 1)
                        dve.wait_ge(s_rs, BU[li] + u + 1)
                        for h in range(2):
                            o = CTX[:].rearrange("p t b c -> p t (b c)")[:, :, bass.ds((u * 2 + h) * D, D)] \
                                .rearrange("p (a c) d -> p c a d", a=2)
                            nc.vector.tensor_tensor(o, px[:, :, h, :, 0:D],
                                                    rs[:, :, h, :].unsqueeze(3).broadcast_to([P, 4, 2, D]),
                                                    ALU.mult).then_inc(s_ctx, 1)
                run(dve, li, do)

            for q in range(G // 4):
                dve.wait_ge(s_wo, q + 1)
                if q == 0:
                    dve.wait_ge(s_xte, 8)
                link(nc.vector.tensor_tensor(X[:, 4 * q:4 * q + 4, :], PMR[q].rearrange("p (t c) -> p t c", t=4),
                                             X1[:, 4 * q:4 * q + 4, :], ALU.add))
            link(nc.vector.tensor_tensor(X[:], X[:], ROWS[:, 4:5, :].broadcast_to([P, G, HS]), ALU.add))
            norm(X, HN2, 3)
            affine(HN2, 2)
            dve.wait_ge(s_gate, 1)
            gb = GB[:].unsqueeze(1).broadcast_to([P, G, E])
            rank = RANK[:].unsqueeze(1).broadcast_to([P, G, E])
            link(nc.vector.tensor_tensor(LG[:], PO[:, 0:G * E].rearrange("p (g e) -> p g e", e=E), gb, ALU.add))
            link(nc.vector.tensor_reduce(LM[:], LG[:], AX_X, ALU.max))
            link(nc.vector.tensor_tensor(LE[:], LG[:], LM[:].unsqueeze(2).broadcast_to([P, G, E]), ALU.is_ge))
            link(nc.vector.tensor_tensor(LE[:], LE[:], rank, ALU.mult))
            link(nc.vector.tensor_reduce(LM[:], LE[:], AX_X, ALU.max))
            nc.vector.tensor_tensor(OH[:], LE[:], LM[:].unsqueeze(2).broadcast_to([P, G, E]),
                                    ALU.is_equal).then_inc(s_oh, 1)
            dve.wait_ge(s_oh, 1)
            dve.wait_ge(s_count, 2)
            dve.wait_ge(s_jc, SLOTS + 1)
            step(nc.vector.tensor_copy(PREF[:], PO[:, 0:G * E].rearrange("p (g e) -> p g e", e=E)))
            step(nc.vector.tensor_copy(TOT[:], PX[:, 0:G * E].rearrange("p (g e) -> p g e", e=E)))
            link(nc.vector.tensor_copy(CUM[0][:], PX[:, 0:G * E].rearrange("p (g e) -> p g e", e=E)))
            a, b_ = CUM
            for d in (1, 2, 4, 8):
                step(nc.vector.tensor_copy(b_[:, 0:d, :], a[:, 0:d, :]))
                link(nc.vector.tensor_tensor(b_[:, d:, :], a[:, d:, :], a[:, :G - d, :], ALU.add))
                a, b_ = b_, a
            cmp_ = CMP[:].rearrange("p s e -> p (s e)")[:, 0:E * G].rearrange("p (e g) -> p e g", e=E)
            link(nc.vector.tensor_tensor(cmp_, a[:, G - 1, :].unsqueeze(2).broadcast_to([P, E, G]),
                                         KC[:].unsqueeze(1).broadcast_to([P, E, G]), ALU.is_gt))
            link(nc.vector.tensor_reduce(TL[:], cmp_, AX_X, ALU.add))
            link(nc.vector.tensor_copy(EN[0][:], TL[:]))
            c, d_ = EN
            for d in (1, 2, 4):
                step(nc.vector.tensor_copy(d_[:, 0:d], c[:, 0:d]))
                link(nc.vector.tensor_tensor(d_[:, d:], c[:, d:], c[:, :E - d], ALU.add))
                c, d_ = d_, c
            link(nc.vector.tensor_tensor(S128[:], c[:], TL[:], ALU.subtract))
            link(nc.vector.tensor_scalar(S128[:], S128[:], float(P), None, ALU.mult))
            link(nc.vector.tensor_tensor(PREF[:], PREF[:], a[:], ALU.add))
            link(nc.vector.tensor_tensor(PREF[:], PREF[:], TOT[:], ALU.subtract))
            link(nc.vector.tensor_tensor(PREF[:], PREF[:], S128[:].unsqueeze(1).broadcast_to([P, G, E]), ALU.add))
            link(nc.vector.tensor_tensor(PREF[:], PREF[:], OH[:], ALU.mult))
            link(nc.vector.tensor_reduce(POSF[:], PREF[:], AX_X, ALU.add))
            nc.vector.tensor_copy(POS[:], POSF[:]).then_inc(s_pos, 1)
            link(nc.vector.tensor_tensor(CMP[:], c[:].unsqueeze(1).broadcast_to([P, SLOTS, E]),
                                         JC[:].unsqueeze(2).broadcast_to([P, SLOTS, E]), ALU.is_le))
            link(nc.vector.tensor_reduce(EJF[:], CMP[:], AX_X, ALU.add))
            nc.vector.tensor_scalar(EJ[:], EJF[:], float(E - 1), None, ALU.min).then_inc(s_pos, 1)
            dve.wait_ge(s_pos, 2)
            link(nc.vector.tensor_tensor(X[:], X[:], X1[:], ALU.add))
            dve.wait_ge(s_wready, 4)
            dve.wait_ge(s_we, 48)
            dve.nop(nofuse=True).then_inc(s_hte, 12)
            dve.nop(nofuse=True).then_inc(s_ye, 3)
            with dve.Fori(0, SLOTS // 3) as r:
                e = [dve.value_load(EJ[0:1, bass.ds(r * 3 + i, 1)], min_val=0, max_val=E - 1) for i in range(3)]
                for i in range(3):
                    n = r * 3 + i
                    dve.wait_ge(s_ht, n + 4)
                    dve.wait_ge(s_y, n + 1)
                    for f in range(FC):
                        nc.vector.tensor_scalar(HT[i][:, f * P:(f + 1) * P], TB[i][:, f * P:(f + 1) * P],
                                                B1T[:, bass.ds(e[i] * FC + f, 1)], 0.0,
                                                ALU.add, ALU.max).then_inc(s_hte, 1)
                for i in range(3):
                    n = r * 3 + i
                    dve.wait_ge(s_y, n + 4)
                    nc.vector.tensor_tensor(YSB[:, bass.ds(n, 1), :], YB[i].unsqueeze(1),
                                            B2A[:, bass.ds(e[i], 1), :], ALU.add).then_inc(s_ye, 1)
            dve.wait_ge(s_back, 16 * G)
            link(nc.vector.tensor_tensor(X[:], X[:], MOE, ALU.add))
            norm(X, X1, 4, s_fin)

        @block.tensor
        def _(pe):
            pe.wait_ge(s_ident, 2)
            pe.wait_ge(s_w, 16 * 9)
            for i in range(3):
                pe.transpose(PX[:, i * P:(i + 1) * P], WRAW[:, i, :], IDF[:]).then_inc(s_wt, 1)

            def transposes(n, src):
                for q in range(G // 4):
                    if q >= 2 or n:
                        pe.wait_ge(s_xte, 4 * n + q - 1)
                    for t in range(4):
                        ins = pe.transpose(PE[q % 2][:, t * P:(t + 1) * P], src(4 * q + t), IDF[:])
                    ins.then_inc(s_xt, 1)

            def project(li):
                if li == 0:
                    pe.wait_ge(s_x, 160)
                else:
                    pe.wait_ge(s_src, 1)
                transposes(li, lambda g: X[:, g, :])
                pe.wait_ge(s_wready, 2 + li)
                w = WQKV if li == 0 else WF
                if li == 1:
                    pe.wait_ge(s_small, 16 * 12)
                for g in range(G):
                    pe.wait_ge(s_xte, 4 * li + g // 4 + 1)
                    if g >= 4:
                        pe.wait_ge(s_proje, 2 * (G * li + g - 3))
                    pe.matmul(PMR[g % 4][:, 0:3 * HS], XT[:, g * P:(g + 1) * P], w[:], start=True,
                              stop=True).then_inc(s_proj, 1)
                pe.wait_ge(s_parts[0], 16 * (li + 1))
                if li == 0:
                    pe.wait_ge(s_const, NCONST)

            for li, L in enumerate(LAYERS):
                project(li)
                shared = PLANS[li][2]

                def shared_free(kind, u0, u, li=li, shared=shared):
                    if shared[kind, u0] is None:
                        return
                    k2, u2 = shared[kind, u0]
                    v = u + (u2 - u0)
                    if k2 == "K":
                        pe.wait_ge(s_k1, BU[li] + v + 1)
                    s, value = {"K": (s_qk, 2 * (BU[li] + v) + 1), "Q": (s_qk, 2 * (BU[li] + v) + 2),
                                "MT": (s_mte, BU[li] + v + 1), "OT": (s_ctx, 2 * (BU[li] + v + 1))}[k2]
                    pe.wait_ge(s, value)

                def do(kind, u0, u, k, li=li, L=L):
                    q, kt, vb = QT[u0 % UB], KT[u0 % UB], VB[u0 % 2]
                    if kind in ("K", "Q"):
                        w = 1 if kind == "K" else 0
                        shared_free(kind, u0, u)
                        if u0 >= UB and kind == "K":
                            pe.wait_ge(s_parts[1], 16 * (li + 1))
                        for t in range(TT):
                            src = QK[:, w, t, :, :, :].rearrange("p b h s -> p (b h s)")[:, bass.ds(u * P, P)]
                            ins = pe.transpose(PXB[:, t * P:(t + 1) * P], src, IDB[:])
                        ins.then_inc(s_trans, 1)
                    if kind == "MAX":
                        st = L.max_steps[k]
                        pm = PM[(u0 * NMX[li] + k) % 2]
                        if k == 0:
                            pe.wait_ge(s_qk, 2 * (BU[li] + u + 1))
                            pe.wait_ge(s_k1, BU[li] + u + 1)
                        count = BM[li] + u * NMX[li] + k
                        wait(pe, s_max, count - 1)
                        for item in st["mms"]:
                            h, m = item if isinstance(item, tuple) else (st["h"], item)
                            (r0, r1), (l0, ln), (c0, cn) = m["rows"], m["left"], m["right"]
                            o = m["bank"] * 512 + m["col"]
                            ins = pe.matmul(pm[r0:r1, o:o + cn], q[:, l0:l0 + ln], kt[:, h, c0:c0 + cn],
                                            start=True, stop=True)
                        ins.then_inc(s_maxmm, 1)
                    if kind == "EXP":
                        count = BX[li] + u * NX[li] + k
                        if k == 0:
                            pe.wait_ge(s_mrow, 32 * (BU[li] + u + 1))
                        wait(pe, s_exp, count - 1)
                        ps = PE[(u0 * NX[li] + k) % 2]
                        for h, m in L.exp_tiles[k]["mms"]:
                            (r0, r1), (l0, ln), (c0, cn) = m["rows"], m["left"], m["right"]
                            ins = pe.matmul(ps[r0:r1, m["col"]:m["col"] + cn], kt[:, h, l0:l0 + ln], q[:, c0:c0 + cn],
                                            start=True, stop=True)
                        ins.then_inc(s_sc, 1)
                    if kind == "AV":
                        gr = L.av_groups[k]
                        pe.wait_ge(s_exp, BX[li] + u * NX[li] + gr["last"] + 1)
                        if k == 0:
                            pe.wait_ge(s_v, (3 * UNITS if li else 0) + len(L.kinds) * (u + 1))
                            wait(pe, s_oe, BU[li] + u)
                        for h, half, e, (c0, cn), kd, t, o, first, last in gr["mms"]:
                            r = 64 * h + 32 * half
                            ins = pe.matmul(PO[r:r + 32, o:o + cn], vb[:, L.kinds.index(kd), t, h, :],
                                            PR[:, e % L.ring, c0:c0 + cn], start=first, stop=last,
                                            skip_group_check=True, tile_position=(0, r))
                        ins.then_inc(s_av, 1)
                    if kind == "MT":
                        shared_free(kind, u0, u)
                        pe.wait_ge(s_split, 4 * (BU[li] + u + 1))
                        pe.nop(nofuse=True)
                        pe.transpose(PXB[0:6 * TT, 0:P], MS[u0 % 2][:].rearrange("p h s t -> p (h s t)"),
                                     IDB[:]).then_inc(s_mt, 1)
                    if kind == "OT":
                        shared_free(kind, u0, u)
                        pe.wait_ge(s_oe, BU[li] + u + 1)
                        for c in range(4):
                            ins = pe.transpose(PX[:, c * P:(c + 1) * P], OS[:, c * P:(c + 1) * P], IDF[:])
                        ins.then_inc(s_ot, 1)

                run(pe, li, do)

            pe.wait_ge(s_ctx, 4 * UNITS)
            transposes(2, lambda g: CTX[:, g % TT, g // TT, :])
            pe.wait_ge(s_max, BM[1] + UNITS * NMX[1])
            for g in range(G):
                pe.wait_ge(s_xte, 8 + g // 4 + 1)
                ins = pe.matmul(PMR[g // 4][:, (g % 4) * P:(g % 4 + 1) * P], XT[:, g * P:(g + 1) * P], WO[:],
                                start=True, stop=True)
                if g % 4 == 3:
                    ins.then_inc(s_wo, 1)
            pe.transpose(PX[:, 0:E * FC], B1R[:], IDF[0:E * FC, 0:E * FC]).then_inc(s_wt, 1)
            pe.wait_ge(s_src, 2)
            transposes(3, lambda g: HN2[:, g, :])
            for g in range(G):
                pe.wait_ge(s_xte, 12 + g // 4 + 1)
                ins = pe.matmul(PO[:, g * E:(g + 1) * E], XT[:, g * P:(g + 1) * P], GW[:], start=True, stop=True)
            ins.then_inc(s_gate, 1)
            pe.wait_ge(s_oh, 1)
            pe.wait_ge(s_tri, 3)
            oh = OH[:].rearrange("p g e -> p (g e)")
            pe.matmul(PO[:, 0:G * E], TRI[:], oh, start=True, stop=True).then_inc(s_count, 1)
            pe.matmul(PX[:, 0:G * E], ONES[:], oh, start=True, stop=True).then_inc(s_count, 1)
            for q in range(SLOTS // 4):
                pe.wait_ge(s_xs[q // 2], 16)
                pe.wait_ge(s_xte, 16 + q - 1)
                for t in range(4):
                    ins = pe.transpose(PE[q % 2][:, t * P:(t + 1) * P], XSB[:, 4 * q + t, :], IDF[:])
                ins.then_inc(s_xt, 1)
            pe.wait_ge(s_xte, 16 + SLOTS // 4)
            pe.wait_ge(s_pos, 2)
            pe.wait_ge(s_we, 48)
            pe.nop(nofuse=True).then_inc(s_ht, 3)
            pe.nop(nofuse=True).then_inc(s_y, 3)
            pe.nop(nofuse=True).then_inc(s_h, 3)
            with pe.Fori(0, SLOTS // 3) as r:
                e = [pe.value_load(EJ[0:1, bass.ds(r * 3 + i, 1)], min_val=0, max_val=E - 1) for i in range(3)]
                for i in range(3):
                    n = r * 3 + i
                    pe.wait_ge(s_he, n + 1)
                    if i == 0:
                        pe.wait_ge(s_ye, n + 3)
                    pe.wait_ge(s_xc, n + 1)
                    pe.matmul(PMR[i], XC[:, i * P:(i + 1) * P], W1A[:, bass.ds(e[i], 1), :].rearrange("p o f -> p (o f)"),
                              start=True, stop=True).then_inc(s_h, 1)
                for i in range(3):
                    n = r * 3 + i
                    pe.wait_ge(s_he, n + 4)
                    pe.wait_ge(s_hte, n * 4 + 4)
                    for f in range(FC):
                        ins = pe.transpose(TB[i][:, f * P:(f + 1) * P], H1[i][:, f * P:(f + 1) * P], IDF[:])
                    ins.then_inc(s_ht, 1)
                for i in range(3):
                    n = r * 3 + i
                    pe.wait_ge(s_hte, n * 4 + 16)
                    pe.wait_ge(s_ye, n + 1)
                    for f in range(FC):
                        ins = pe.matmul(YB[i], HT[i][:, f * P:(f + 1) * P],
                                        W2A[:, bass.ds(e[i] * FC + f, 1), :].rearrange("p o n -> p (o n)"),
                                        start=(f == 0), stop=(f == FC - 1))
                    ins.then_inc(s_y, 1)


_INS = ['hidden_states', 'Wq', 'bq', 'Wk', 'bk', 'Wv', 'bv']
_FFN = ['ln1_g', 'ln1_b', 'ln2_g', 'ln2_b', 'wq', 'bq', 'wk', 'bk', 'wv', 'bv', 'wo', 'bo', 'gate_w', 'gate_b',
        'w1', 'b1', 'w2', 'b2']
_NAMES = ['L0_attn_' + n for n in _INS] + ['L0_ffn_' + n for n in _FFN]


def kernel(**inputs):
    import numpy as _np
    import concourse.bacc as _bacc
    from concourse import mybir as _mybir
    from concourse.bass_utils import run_bass_kernel_spmd as _run

    nc = _bacc.Bacc("TRN2", target_bir_lowering=False, num_devices=1)
    arrays, args = {}, []
    for name in _NAMES:
        a = _np.ascontiguousarray(inputs[name])
        arrays[f"in_{name}_dram"] = a
        args.append(nc.dram_tensor(f"in_{name}_dram", a.shape, _mybir.dt.from_np(a.dtype), kind="ExternalInput").ap())
    args.append(nc.dram_tensor("out_0_dram", (B, SEQ, HS), F32, kind="ExternalOutput").ap())
    build(nc, *args)
    r = _run(nc, [arrays], core_ids=[0])
    return r.results[0]["out_0_dram"]
```

```python
from contextlib import ExitStack

import numpy as np

import concourse.bass as bass
from concourse import mybir

ALU = mybir.AluOpType
ACT = mybir.ActivationFunctionType
AX_X = mybir.AxisListType.X
F32 = mybir.dt.float32
I32 = mybir.dt.int32
BF16 = mybir.dt.bfloat16

P = 128
B, SEQ, HS = 2, 1024, 128
H, D = 16, 8
BLK = 64
TT = SEQ // P
G = B * TT
E, F = 8, 512
FC = F // P
PAIRS = H // 2
UNITS = B * PAIRS
DVE_SHARE = 5
SLOTS = G + E
UB = 4
ROW = HS + 1
ROUND = 4
MOE_ORDER = [("w1", 0), ("w1", 1), ("w1", 2), ("w2", 0), ("w1", 3), ("w2", 1), ("w2", 2), ("w2", 3)]
W2_AT, B2_AT, B1_AT = F, F + FC * HS, F + FC * HS + HS
WEXP = B1_AT + FC
SLOT = 64
MROW = 6 * D
SCALE = float(np.float32(1.0 / np.sqrt(D)))
EPS = 1e-5
ROOT_STEPS = 3
HI, MID, LO = (0, 0), (3, 1), (5, 2)
AGAIN = ((0, 1, 0), (0, 2, 0), (0, 4, 3), (1, 3, 0), (1, 5, 0), (1, 4, 1))


def block_col(i):
    return BLK * {0: 0, SEQ // BLK - 1: 1, 1: SEQ // BLK - 1}.get(i, i)


def mm(bank, rows, col, left, right):
    return dict(bank=bank, rows=rows, col=col, left=left, right=right)


ALL, LOW, UPP = (0, P), (0, BLK), (BLK, P)


class Layer:
    pass


def full_layer():
    L = Layer()
    L.slots = 4 * TT
    L.max_steps = [
        dict(h=h, mms=[mm(k, ALL, 0, (t * P, P), (k * 512, 512)) for k in range(2)],
             view=("flat", 1024), out=(h * TT + t, 1, 1))
        for h in range(2) for t in range(TT)]
    L.max_slot = [2 * m for m in range(2 * TT)]
    L.exp_tiles = [
        dict(n=512, mms=[(h, mm(0, ALL, 0, (kt * P, P), (half * 512, 512)))])
        for kt in range(TT) for h in range(2) for half in range(2)]
    L.ring = 8
    L.av_groups = [
        dict(last=4 * kt + 3,
             mms=[(h, half, 4 * kt + 2 * h + half, (0, 512), "full", kt, 0)
                  for h in range(2) for half in range(2)])
        for kt in range(TT)]
    L.av_slot = [4 * g + 5 for g in range(TT)]
    L.kinds = ["full"]
    L.at = dict(MT=2, OT=9, K=14, Q=7, V=16)
    L.lead, L.cut, L.late = 12, 142, dict(K=7, V=5)
    return L


def block_layer():
    L = Layer()
    L.slots = 13
    L.max_steps = []
    for h in range(2):
        L.max_steps.append(dict(h=h, mms=[mm(k, ALL, 0, (0, P), (k * 512, 512)) for k in range(2)],
                                view=("flat", 1024), out=(h * TT, 1, 1)))
        for j0 in (1, 3, 5):
            mms = []
            for k in range(2):
                j = j0 + k
                mms += [mm(k, ALL, 0, (j * P, P), (0, P)),
                        mm(k, ALL, P, (j * P, P), (j * P, P)),
                        mm(k, LOW, 2 * P, (j * P, BLK), (block_col(2 * j - 1), BLK)),
                        mm(k, UPP, 2 * P, (j * P + BLK, BLK), (block_col(2 * j + 2), BLK))]
            L.max_steps.append(dict(h=h, mms=mms, view=("banks", 320), out=(h * TT + j0, 2, 1)))
    t7 = (TT - 1) * P
    mms = []
    for h in range(2):
        mms += [(h, mm(h, ALL, 0, (t7, P), (0, P))),
                (h, mm(h, LOW, P, (t7, BLK), (block_col(13), P))),
                (h, mm(h, UPP, P, (t7 + BLK, BLK), (block_col(1), BLK))),
                (h, mm(h, UPP, P + BLK, (t7 + BLK, BLK), (block_col(2), BLK)))]
    L.max_steps.append(dict(h=None, mms=mms, view=("banks", 256), out=(TT - 1, 2, TT)))
    L.max_slot = [0, 2, 3, 4, 6, 7, 9, 10, 12]

    def single(j, col):
        return [mm(0, LOW, col, (block_col(2 * j + 2), BLK), (j * P + BLK, BLK)),
                mm(0, UPP, col, (block_col(2 * j - 1), BLK), (j * P, BLK))]

    def single_v(h, e, j, col):
        q0, q1 = j * P, j * P + BLK
        return [(h, q0 // 512, e, (col, BLK), "upp", block_col(2 * j - 1) // P, q0 % 512),
                (h, q1 // 512, e, (col, BLK), "low", block_col(2 * j + 2) // P, q1 % 512)]

    t1, t6 = block_col(2) // P, block_col(13) // P
    tiles, groups = [], []
    for kind in range(6):
        group = dict(last=2 * kind + 1, mms=[])
        per_head = []
        for h in range(2):
            e, v = 2 * kind + h, []
            if kind < 2:
                ts = range(4 * kind, 4 * kind + 4)
                mms = [mm(0, ALL, i * P, (t * P, P), (0, P)) for i, t in enumerate(ts)]
                v = [(h, 0, e, (i * P, P), "full", t, 0) for i, t in enumerate(ts)]
                n = 512
            elif kind == 2:
                mms = [mm(0, ALL, 0, (0, P), (P, 512))]
                v = [(h, 0, e, (0, 384), "full", 0, P), (h, 1, e, (384, P), "full", 0, 0)]
                n = 512
            elif kind == 3:
                mms = [mm(0, ALL, 0, (0, P), (640, 384)),
                       mm(0, LOW, 384, (block_col(14), BLK), (t7, BLK)),
                       mm(0, UPP, 384, (block_col(13), BLK), (t7, BLK)),
                       mm(0, LOW, 448, (block_col(2), BLK), (t7 + BLK, BLK)),
                       mm(0, UPP, 448, (block_col(1), BLK), (t7 + BLK, BLK))]
                v = [(h, 1, e, (0, 384), "full", 0, P),
                     (h, 1, e, (384, BLK), "low", TT - 1, 384), (h, 1, e, (384, BLK), "upp", t6, 384),
                     (h, 1, e, (448, BLK), "low", t1, 448), (h, 1, e, (448, BLK), "upp", TT - 1, 448)]
                n = 512
            elif kind == 4:
                mms = [mm(0, ALL, (j - 1) * P, (j * P, P), (j * P, P)) for j in range(1, 5)]
                v = [(h, j // 4, e, ((j - 1) * P, P), "full", j, j % 4 * P) for j in range(1, 5)]
                n = 512
            else:
                mms = [mm(0, ALL, (j - 5) * P, (j * P, P), (j * P, P)) for j in (5, 6)]
                v = [(h, 1, e, ((j - 5) * P, P), "full", j, j % 4 * P) for j in (5, 6)]
                for j in range(1, 5):
                    mms += single(j, 256 + (j - 1) * BLK)
                    v += single_v(h, e, j, 256 + (j - 1) * BLK)
                n = 512
            tiles.append(dict(n=n, mms=[(h, m) for m in mms]))
            per_head.append(v)
        for a, b in zip(*per_head):
            group["mms"] += [a, b]
        groups.append(group)
    mms, per_head = [], []
    for h in range(2):
        v = []
        for j in (5, 6):
            col = h * P + (j - 5) * BLK
            mms += [(h, m) for m in single(j, col)]
            v += single_v(h, 12, j, col)
        per_head.append(v)
    tiles.append(dict(n=2 * P, mms=mms))
    groups.append(dict(last=12, mms=[x for pair in zip(*per_head) for x in pair]))
    L.exp_tiles, L.av_groups = tiles, groups
    L.ring = len(tiles)
    L.av_slot = [2 * g + 3 for g in range(6)] + [14]
    L.kinds = ["full", "low", "upp"]
    L.at = dict(MT=3, OT=5, K=7, Q=4, V=8)
    L.lead, L.cut, L.late = 10, 20, dict(K=4, V=2)
    return L


def mark_ends(L):
    flat = [(g, i, m[:2]) for g, gr in enumerate(L.av_groups) for i, m in enumerate(gr["mms"])]
    first, last = {}, {}
    for g, i, key in flat:
        first.setdefault(key, (g, i))
        last[key] = (g, i)
    for g, gr in enumerate(L.av_groups):
        gr["mms"] = [m + (first[m[:2]] == (g, i), last[m[:2]] == (g, i)) for i, m in enumerate(gr["mms"])]
    return L


def unit_acts(L, li):
    S, acts = L.slots, []
    for u in range(UNITS):
        acts += [(u * S + e, 0, "EXP", u, e) for e in range(len(L.exp_tiles))]
        t0 = (u - 1) * S - L.lead
        acts += [(t0 + s, 1, "MAX", u, m) for m, s in enumerate(L.max_slot)]
        acts += [(u * S + s, 2, "AV", u, g) for g, s in enumerate(L.av_slot)]
        acts += [(u * S + L.av_slot[-1], 3, "OE", u, 0)]
        acts += [(t0 + S + L.at["MT"], 4, "MT", u, 0), ((u + 1) * S + L.at["OT"], 5, "OT", u, 0)]
        acts += [((u - 1) * S + L.at["V"], 8, "V", u, 0)]
        acts += [(t0 - L.at["K"], 6, "K", u, 0), (t0 - L.at["Q"], 7, "Q", u, 0)]
    return [(t, p, kind, li, u, k) for t, p, kind, u, k in acts]


QKV_STEPS = [("XT", 0, 0), ("XT", 1, 2)] + [("PJ", t, 3 + t) for t in range(TT)] + \
    [("PART", (0, 0), 8), ("PART", (0, 1), 9), ("PART", (1, 0), 11), ("PART", (0, 2), 12), ("LO", (0, 0), 14),
     ("LO", (0, 1), 15), ("PART", (1, 1), 13), ("PART", (1, 2), 16), ("LO", (1, 0), 18), ("LO", (1, 1), 19)]
NORM_STEPS = [("RES", 0, 0)] + [("SUM", (0, i), 2 + i) for i in range(TT // 2)] + [("ROOT", 0, 5)] + \
    [("SCALE", (0, i), 8 + i) for i in range(TT // 2)] + [("SUM", (1, i), 10 + i) for i in range(TT // 2)] + \
    [("ROOT", 1, 14)] + [("SCALE", (1, i), 16 + i) for i in range(TT // 2)] + [("AFFINE", 0, 18), ("AFFINE", 1, 19)]


POST_STEPS = [("CT", 0, 0), ("CT", 1, 2), ("WO", 0, 4), ("WO", 1, 6)] + \
    [("SUM", (0, i), 8 + i) for i in range(TT // 2)] + [("ROOT", 0, 12)] + \
    [("SCALE", (0, i), 14 + i) for i in range(TT // 2)] + [("AFFINE", 0, 16), ("AFFINE", 1, 18), ("NT", 0, 20),
                                                           ("NT", 1, 22), ("GATE", 0, 24)]


def between(steps, li, b, t0, pace):
    return [(t0 + pace * t, 9, kind, li, b, k) for kind, k, t in steps]


def plan(layers):
    A, F = layers
    RA, RF = 4, 3
    t_f = UNITS * A.slots * RA + 52
    acts = [(RA * a[0],) + a[1:] for a in unit_acts(A, 0)]
    acts += [(t_f + RF * a[0],) + a[1:] for a in unit_acts(F, 1)]
    acts += between(QKV_STEPS, 0, 1, -12 * RA, 6)
    half = PAIRS * A.slots * RA
    acts += between(NORM_STEPS, 1, 0, half + 20 * RA, 4)
    acts += between(QKV_STEPS, 1, 0, half + 40 * RA, 5)
    acts += between(NORM_STEPS, 1, 1, t_f + 12 * RF, 10)
    acts += between(QKV_STEPS, 1, 1, t_f + 80 * RF, 9)
    acts += between(POST_STEPS, 2, 0, t_f + (UNITS - 1) * F.slots * RF - 16 * RF, 5)
    acts += between(POST_STEPS, 2, 1, t_f + (UNITS + 2) * F.slots * RF, 1)
    acts.sort()
    for kind in ("K", "Q", "MAX", "MT", "EXP", "AV", "OE", "OT", "V"):
        mine = [a[3:] for a in acts if a[2] == kind]
        assert mine == sorted(mine)
    shared, before = {}, None
    for _, _, kind, li, u, k in acts:
        if kind in ("K", "Q", "MT", "OT", "XT", "PJ", "CT", "WO", "NT", "GATE"):
            shared[kind, li, u, k] = before
            before = (kind, li, u, k)
    parts, start, rounds = [], -10 ** 9, 2
    for L, r, t0 in ((A, RA, 0), (F, RF, t_f)):
        lo, span = t0 + r * L.cut, r * UB * L.slots
        parts.append((start, lo, 0))
        body = [a for a in acts if lo <= a[0] < lo + span]
        for i in range(1, rounds):
            again = [(t + i * span, p, kind, li, u + i * UB, x) for t, p, kind, li, u, x in body]
            assert again == [a for a in acts if lo + i * span <= a[0] < lo + (i + 1) * span]
            first = [a[2:] for a in body if a[2:] in shared][0]
            assert shared[first][0] == shared[again[[a[2:] for a in body].index(first)][2:]][0]
        parts.append((lo, lo + span, rounds))
        start = lo + rounds * span
    parts.append((start, 10 ** 9, 0))
    return [([a[2:] for a in acts if lo <= a[0] < hi], rounds) for lo, hi, rounds in parts], shared


def build(nc, x, Wq, bq, Wk, bk, Wv, bv, ln1_g, ln1_b, ln2_g, ln2_b, fwq, fbq, fwk, fbk, fwv, fbv, fwo, fbo,
          gate_w, gate_b, w1, b1, w2, b2, out):
    LAYERS = [mark_ends(block_layer()), mark_ends(full_layer())]
    PARTS, SHARED = plan(LAYERS)
    with ExitStack() as ctx:
        def sb(name, shape, dt=F32):
            return ctx.enter_context(nc.sbuf_tensor(name, shape, dt))

        def pb(name, shape, dt=F32):
            return ctx.enter_context(nc.psum_tensor(name, shape, dt))

        def sem(name):
            return ctx.enter_context(nc.semaphore(name))

        X = sb("X", [P, G, HS])
        X1 = sb("X1", [P, G, HS])
        CTX = sb("CTX", [P, TT, B, H * D])
        XT = sb("XT", [P, G * P])
        QKV = sb("QKV", [P, G, 2 * HS])
        VST = sb("VST", [P, TT, B, H * D])
        QK = sb("QK", [P, 2, TT, B, H, SLOT], BF16)
        WQKV = sb("WQKV", [P, 3 * HS])
        WF = sb("WF", [P, 3 * HS])
        BIAS = sb("BIAS", [P, 2, 3 * HS])
        WO = sb("WO", [P, HS])
        GW = sb("GW", [P, E])
        ROWS = sb("ROWS", [P, 5, HS])
        GB = sb("GB", [P, E])
        B1R = sb("B1R", [E * FC, P])
        IDF = sb("IDF", [P, P])
        IDB = sb("IDB", [P, P], BF16)
        QT = [sb(f"QT{i}", [P, SEQ], BF16) for i in range(UB)]
        KT = [sb(f"KT{i}", [P, 2, SEQ], BF16) for i in range(UB)]
        VB = [sb(f"VB{i}", [P, 3, TT, 2, 32]) for i in range(2)]
        PR = sb("PR", [P, 13, 512])
        NM = [sb(f"NM{i}", [P, 2 * TT]) for i in range(2)]
        NR = [sb(f"NR{i}", [P, 2 * TT]) for i in range(2)]
        MS = [sb(f"MS{i}", [P, 2, 3, TT], BF16) for i in range(2)]
        MT = [sb(f"MT{i}", [6 * TT, P], BF16) for i in range(2)]
        OS = sb("OS", [P, 512])
        WRAW = OS[:, 0:3 * HS].rearrange("p (i c) -> p i c", i=3)
        RS = sb("RS", [P, 2 * TT])
        ST = sb("ST", [P, G, 6])
        MV = sb("MV", [P, G, 2])
        VE = sb("VE", [P, G])
        SD = sb("SD", [P, G])
        RD = sb("RD", [P, G])
        NMR = sb("NMR", [P, G])
        LG = sb("LG", [P, G, E])
        LE = sb("LE", [P, G, E])
        LM = sb("LM", [P, G])
        OH = sb("OH", [P, G, E])
        RANK = sb("RANK", [P, E])
        PREF = sb("PREF", [P, G, E])
        CUM = [sb(f"CUM{i}", [P, G, E]) for i in range(2)]
        TOT = sb("TOT", [P, G, E])
        TL = sb("TL", [P, E])
        EN = [sb(f"EN{i}", [P, E]) for i in range(2)]
        S128 = sb("S128", [P, E])
        POSF = sb("POSF", [P, G])
        POS = sb("POS", [P, G], mybir.dt.uint32)
        EJF = sb("EJF", [P, SLOTS])
        EJ = sb("EJ", [P, SLOTS], mybir.dt.int32)
        CMP = sb("CMP", [P, SLOTS, E])
        JC = sb("JC", [P, SLOTS])
        KC = sb("KC", [P, G])
        TRI = sb("TRI", [P, P])
        ONES = sb("ONES", [P, P])
        free = QK[:].rearrange("p w t b h s -> p (w t b h s)").bitcast(F32)
        WA = free[:, 0:E * WEXP].rearrange("p (e w) -> p e w", e=E)
        o = E * WEXP
        XSB = free[:, o:o + SLOTS * ROW].rearrange("p (s n) -> p s n", n=ROW)
        o += SLOTS * ROW
        WC = [free[:, o + i * WEXP:o + (i + 1) * WEXP] for i in range(3)] + \
            [PR[:, 0:3, :].rearrange("p a b -> p (a b)")[:, 0:WEXP]]
        o += 3 * WEXP
        YT = [free[:, o + i * HS:o + (i + 1) * HS] for i in range(ROUND)]
        HT = [PR[:, i, :] for i in (3, 4, 5, 12)]
        XST = PR[:, 6:6 + SLOTS // 4, :].rearrange("p a b -> p (a b)")
        IDS = sb("IDS", [P, SLOTS], mybir.dt.uint32)
        SPARE = sb("SPARE", [P, ROUND])
        ID1 = [sb(f"ID1{i}", [P, 1], mybir.dt.uint32) for i in range(ROUND)]
        MOE = CTX[:].rearrange("p t b c -> p (t b) c")
        ZERO = PR[:].rearrange("p a b -> p (a b)")[:, 0:8 * ROW]
        XS = nc.dram_tensor("sorted_rows", (SLOTS * P, ROW), F32).ap()
        YS = nc.dram_tensor("results", (ROUND * P + G * P, HS), F32).ap()
        HN2 = QKV[:].rearrange("p g c -> p (g c)")[:, 0:G * ROW].rearrange("p (g c) -> p g c", g=G)

        PM = [pb(f"PM{i}", [P, 1024]) for i in range(2)]
        PE = [pb(f"PE{i}", [P, 512]) for i in range(2)]
        PO = pb("PO", [P, 512])
        PX = pb("PX", [P, 512])
        PXB = PX[:].bitcast(BF16)
        YB = [PE[0][:, 0:HS], PE[1][:, 0:HS], PM[0][:, 0:HS], PM[0][:, 512:512 + HS]]
        TB = [PX, PO, PM[1][:, 512:1024], PM[1][:, 0:512]]
        PMR = [PM[i // 2][:, 512 * (i % 2):512 * (i % 2) + 512] for i in range(4)]

        s_x = [sem(f"s_x{b}") for b in range(B)]; s_w = sem("s_w"); s_b = sem("s_b")
        s_ktz = sem("s_ktz"); s_small = sem("s_small"); s_out = sem("s_out")
        s_ident = sem("s_ident"); s_init = sem("s_init"); s_const = sem("s_const"); s_rank = sem("s_rank")
        s_wt = sem("s_wt"); s_wready = sem("s_wready"); s_bscaled = sem("s_bscaled")
        s_src = sem("s_src")
        s_xt = sem("s_xt"); s_xte = sem("s_xte")
        s_proj = sem("s_proj"); s_proje = sem("s_proje")
        s_part = sem("s_part"); s_rem = [sem(f"s_rem{b}") for b in range(B)]
        s_parts = [sem(f"s_parts{b}") for b in range(B)]
        s_trans = sem("s_trans"); s_qk = sem("s_qk"); s_k1 = sem("s_k1")
        s_maxmm = sem("s_maxmm"); s_max = sem("s_max"); s_split = sem("s_split")
        s_mt = sem("s_mt"); s_mte = sem("s_mte"); s_mrow = sem("s_mrow")
        s_sc = sem("s_sc"); s_exp = sem("s_exp"); s_v = sem("s_v")
        s_av = sem("s_av"); s_oe = sem("s_oe"); s_ot = sem("s_ot"); s_rs = sem("s_rs"); s_ctx = sem("s_ctx")
        s_dve = sem("s_dve")
        s_var = sem("s_var"); s_stat = sem("s_stat"); s_norm = sem("s_norm")
        s_res = sem("s_res"); s_newton = sem("s_newton"); s_aff = sem("s_aff")
        s_wo = sem("s_wo"); s_woe = sem("s_woe"); s_lg = sem("s_lg"); s_gate = sem("s_gate"); s_oh = sem("s_oh")
        s_count = sem("s_count"); s_pos = sem("s_pos"); s_zero = sem("s_zero"); s_zeroed = sem("s_zeroed")
        s_tri = sem("s_tri"); s_jc = sem("s_jc"); s_we = sem("s_we"); s_scat = sem("s_scat")
        s_xs = [sem(f"s_xs{i}") for i in range(SLOTS // 8)]
        s_wc = sem("s_wc"); s_h = sem("s_h"); s_hte = sem("s_hte"); s_ids = sem("s_ids")
        s_y = sem("s_y"); s_ye = sem("s_ye"); s_id = sem("s_id")
        s_back = [sem(f"s_back{i}") for i in range(ROUND)]; s_moe = [sem(f"s_moe{b}") for b in range(B)]
        s_fin = sem("s_fin"); s_fin1 = sem("s_fin1")

        NCONST = 3 * TT + E
        NX = [len(L.exp_tiles) for L in LAYERS]
        NMX = [len(L.max_steps) for L in LAYERS]
        NAV = [len(L.av_groups) for L in LAYERS]
        BX = [0, UNITS * NX[0]]
        BM = [0, UNITS * NMX[0]]
        BA = [0, UNITS * NAV[0]]
        BU = [0, UNITS]

        def wait(eng, s, value):
            if not (isinstance(value, int) and value <= 0):
                eng.wait_ge(s, value)

        def run(eng, do):
            for acts, rounds in PARTS:
                if not rounds:
                    for kind, li, u, k in acts:
                        do(kind, li, u, u, k)
                else:
                    with eng.Fori(0, rounds) as r:
                        for kind, li, u, k in acts:
                            do(kind, li, u, r * UB + u, k)

        def part(w, t0, b, place):
            return QK[:, w, t0:t0 + 4, b, :, place * D:(place + 1) * D]

        def rest(q, w):
            return QKV[:, 4 * q:4 * q + 4, w * HS:(w + 1) * HS].rearrange("p t (h d) -> p t h d", d=D)

        PART_ORDER = {0: [(0, 0), (1, 0), (0, 2), (1, 2)]}
        for b_ in (1, 2, 3):
            PART_ORDER[b_] = [k for kind, k, _ in QKV_STEPS if kind == "PART" and k[1] in (0, 2)]

        def part_count(li, b, k):
            return 2 * (4 * (2 * li + b) + PART_ORDER[2 * li + b].index(k) + 1)

        def root_steps(eng, ops, s, before, v, y, t):
            for i in range(ROOT_STEPS):
                for j, ins in enumerate((lambda: ops.tensor_tensor(t, y, y, ALU.mult),
                                         lambda: ops.tensor_tensor(t, t, v, ALU.mult),
                                         lambda: ops.tensor_scalar(t, t, -0.5, 1.5, ALU.mult, ALU.add),
                                         lambda: ops.tensor_tensor(y, y, t, ALU.mult))):
                    ins().then_inc(s, 1)
                    eng.wait_ge(s, before + 4 * i + j + 1)

        def exp_bank(li, u0, u, k):
            if li == 1 and isinstance(u, int) and u == UNITS - 1:
                return ([PE[0][:], PE[1][:]] + PMR)[k % 6]
            return PE[(u0 * NX[li] + k) % 2][:]

        def post_count(kind, u, k):
            return 8 + 4 * u + (2 if kind == "NT" else 0) + k + 1

        def kt_free(eng, li, u):
            if isinstance(u, int) and u < UB:
                wait(eng, s_sc, BX[li] + (u - UB + 1) * NX[0])
            else:
                eng.wait_ge(s_sc, BX[li] + (u - UB + 1) * NX[li])

        block = ctx.enter_context(nc.Block())

        @block.sync
        def _(sp):
            for i, w in enumerate((Wq, Wk, Wv)):
                sp.dma_start(WRAW[:, i, :], w[:, :]).then_inc(s_w, 16)
            def load_x(b):
                xb = x[b]
                g = b * TT
                sp.dma_start(X[:, g + 1:g + 7, :], xb[P:7 * P, :].rearrange("(j p) c -> p j c", p=P)).then_inc(s_x[b], 16)
                for t, half, blk in ((0, 0, 0), (0, 1, 15), (7, 0, 14), (7, 1, 1)):
                    sp.dma_start(X[half * BLK:(half + 1) * BLK, g + t, :],
                                 xb[blk * BLK:(blk + 1) * BLK, :]).then_inc(s_x[b], 16)
            load_x(0)
            for i, v in enumerate((bq, bk, bv, fbq, fbk, fbv)):
                sp.dma_start(BIAS[:, i // 3, (i % 3) * HS:(i % 3 + 1) * HS], v.partition_broadcast(P)).then_inc(s_b, 16)
            load_x(1)
            for i, w in enumerate((fwq, fwk, fwv)):
                sp.dma_start(WF[:, i * HS:(i + 1) * HS], w[:, :]).then_inc(s_small, 16)
            sp.dma_start(WO[:], fwo[:, :]).then_inc(s_small, 16)
            sp.dma_start(GW[:], gate_w[:, :]).then_inc(s_small, 16)
            sp.dma_start(GB[:], gate_b.partition_broadcast(P)).then_inc(s_small, 16)
            for i, v in enumerate((ln1_g, ln1_b, ln2_g, ln2_b, fbo)):
                sp.dma_start(ROWS[:, i, :], v.partition_broadcast(P)).then_inc(s_small, 16)
            sp.dma_start(B1R[:], b1.rearrange("e (c f) -> (e c) f", f=P)).then_inc(s_small, 16)
            sp.wait_ge(s_zero, 1)
            for i in range(SLOTS // 8):
                sp.dma_start(XS[i * 8 * P:(i + 1) * 8 * P, :].rearrange("(s p) n -> p s n", p=P),
                             ZERO.rearrange("p (s n) -> p s n", n=ROW)).then_inc(s_zeroed, 16)

            def do(kind, li, u0, u, k):
                if kind == "MT":
                    sp.wait_ge(s_mte, BU[li] + u + 1)
                    for h in range(2):
                        row = h * SLOT + MROW
                        sp.dma_start(QT[u0 % UB][row:row + 3, :].rearrange("s (t q) -> s t q", t=TT),
                                     MT[u0 % 2][h * 3 * TT:(h + 1) * 3 * TT, :]).then_inc(s_mrow, 16)
            run(sp, do)

            sp.wait_ge(s_trans, 4 * UNITS)
            sp.dma_start(WA[:, :, 0:F], w1.rearrange("e h f -> h e f")).then_inc(s_we, 16)
            for c in range(FC):
                sp.dma_start(WA[:, :, W2_AT + c * HS:W2_AT + (c + 1) * HS],
                             w2[:, c * P:(c + 1) * P, :].rearrange("e f n -> f e n")).then_inc(s_we, 16)
            sp.dma_start(WA[:, :, B2_AT:B1_AT], b2.rearrange("e n -> (e n)").partition_broadcast(P)
                         .rearrange("p (e n) -> p e n", n=HS)).then_inc(s_we, 16)
            sp.wait_ge(s_scat, 16 * G)
            for i in range(SLOTS // 8):
                sp.dma_start(XSB[:, 8 * i:8 * i + 8, :],
                             XS[i * 8 * P:(i + 1) * 8 * P, :].rearrange("(s p) n -> p s n", p=P)).then_inc(s_xs[i], 16)
            for i in range(ROUND):
                sp.wait_ge(s_back[i], 16 * (SLOTS // ROUND + 1))
            for b in range(B):
                sp.dma_start(MOE[:, b * TT:(b + 1) * TT, :],
                             YS[ROUND * P + b * SEQ:ROUND * P + (b + 1) * SEQ, :].rearrange("(t p) n -> p t n", p=P)
                             ).then_inc(s_moe[b], 16)

            for b in range(B):
                g = b * TT
                sp.wait_ge(s_fin, (b + 1) * TT - (DVE_SHARE if b == B - 1 else 0))
                if b == B - 1:
                    sp.wait_ge(s_fin1, DVE_SHARE)
                ob = out[b]
                sp.dma_start(ob[P:7 * P, :].rearrange("(j p) c -> p j c", p=P), X1[:, g + 1:g + 7, :]).then_inc(s_out, 16)
                for t, half, blk in ((0, 0, 0), (0, 1, 15), (7, 0, 14), (7, 1, 1)):
                    sp.dma_start(ob[blk * BLK:(blk + 1) * BLK, :],
                                 X1[half * BLK:(half + 1) * BLK, g + t, :]).then_inc(s_out, 16)
            sp.wait_ge(s_out, 16 * 5 * B)

        @block.gpsimd
        def _(pool):
            nc.gpsimd.memset(IDF[:], 0.0).then_inc(s_rank, 1)
            nc.gpsimd.memset(IDB[:], 0.0).then_inc(s_rank, 1)
            pool.wait_ge(s_rank, 2)
            for t in (IDF, IDB):
                nc.gpsimd.affine_select(out=t[:], in_=t[:], compare_op=ALU.not_equal, fill=1.0, base=0,
                                        pattern=[[-1, P]], channel_multiplier=1).then_inc(s_ident, 1)
            for i in range(UB):
                nc.gpsimd.memset(KT[i][:], 0.0).then_inc(s_ktz, 1)
            nc.gpsimd.memset(ONES[:], 1.0).then_inc(s_tri, 1)
            nc.gpsimd.memset(TRI[:], 1.0).then_inc(s_tri, 1)
            pool.wait_ge(s_tri, 2)
            nc.gpsimd.affine_select(out=TRI[:], in_=TRI[:], compare_op=ALU.is_gt, fill=0.0, base=0,
                                    pattern=[[1, P]], channel_multiplier=-1).then_inc(s_tri, 1)
            for j in range(SLOTS):
                nc.gpsimd.memset(JC[:, j:j + 1], float(j)).then_inc(s_jc, 1)
            pool.wait_ge(s_jc, SLOTS)
            nc.gpsimd.tensor_scalar(KC[:], JC[:, 0:G], float(P), None, ALU.mult).then_inc(s_jc, 1)
            pool.wait_ge(s_ident, 2)
            n = 0
            for i in range(2):
                for kind, rows in enumerate((ALL, ALL, LOW, UPP)):
                    if kind == 0:
                        nc.gpsimd.memset(VB[i][:], 0.0).then_inc(s_init, 1)
                    else:
                        nc.gpsimd.memset(VB[i][rows[0]:rows[1], kind - 1, :, :, D:D + 1], 1.0).then_inc(s_init, 1)
                    n += 1
                    pool.wait_ge(s_init, n)

            def do(kind, li, u0, u, k):
                L = LAYERS[li] if li < 2 else None
                if kind == "RES":
                    pool.wait_ge(s_x[u], 16 * 5)
                    pool.wait_ge(s_ctx, 2 * PAIRS * (u + 1))
                    xb = X[:, u * TT:(u + 1) * TT, :]
                    nc.gpsimd.tensor_tensor(xb, xb, CTX[:, :, u, :], ALU.add).then_inc(s_res, 1)
                if kind == "ROOT" and (li, u) != (2, 1):
                    n = 2 * u + k if li == 1 else 4 + u
                    pool.wait_ge(s_var, n + 1)
                    root_steps(pool, nc.gpsimd, s_newton, 4 * ROOT_STEPS * n, VE[:, 0:TT], RD[:, 0:TT], SD[:, 0:TT])
                if kind == "AFFINE" and (li, u) != (2, 1):
                    n, row = (2 * u + 1, 0) if li == 1 else (4 + u, 2)
                    if li == 1 and u == 0:
                        pool.wait_ge(s_small, 16 * 12)
                    pool.wait_ge(s_norm, TT * n + 4 * k + 4)
                    xb = (X[:] if li == 1 else HN2[:, :, 0:HS])[:, u * TT + 4 * k:u * TT + 4 * k + 4, :]
                    nc.gpsimd.tensor_tensor(xb, xb, ROWS[:, row:row + 1, :].broadcast_to([P, 4, HS]),
                                            ALU.mult).then_inc(s_aff, 1)
                    pool.wait_ge(s_aff, 4 * (li - 1) + 2 * u + k + 1)
                    nc.gpsimd.tensor_tensor(xb, xb, ROWS[:, row + 1:row + 2, :].broadcast_to([P, 4, HS]),
                                            ALU.add).then_inc(s_src, 1)
                if kind == "PART" and k[1] == 1:
                    q = 2 * u + k[0]
                    pool.wait_ge(s_proje, 2 * (G * li + 4 * q + 4))
                    pool.wait_ge(s_part, part_count(li, u, (k[0], 0)))
                    for w in range(2):
                        nc.gpsimd.tensor_tensor(rest(q, w), rest(q, w), part(w, 4 * k[0], u, HI[w]),
                                                ALU.subtract).then_inc(s_rem[u], 1)
                if kind == "V":
                    pool.wait_ge(s_proje, 2 * (G * li + (G if u0 >= L.late["V"] else TT)))
                    wait(pool, s_av, (u - 1) * NAV[li] + BA[li] if not isinstance(u, int) or u >= 2
                         else BA[li] + (u - 1) * NAV[0])
                    src = VST[:].rearrange("p t b c -> p t (b c)")[:, :, bass.ds(u * 2 * D, 2 * D)] \
                        .rearrange("p t (h d) -> p t h d", h=2)
                    pool.nop(nofuse=True)
                    for i, kd in enumerate(L.kinds):
                        lo, hi = {"full": ALL, "low": LOW, "upp": UPP}[kd]
                        nc.gpsimd.tensor_copy(VB[u0 % 2][lo:hi, i, :, :, 0:D], src[lo:hi]).then_inc(s_v, 1)
                        pool.wait_ge(s_v, (3 * UNITS if li else 0) + u * len(L.kinds) + (i + 1))
                        pool.nop(nofuse=True)
                if kind == "MT":
                    a, r, m = NM[u0 % 2], NR[u0 % 2], MS[u0 % 2]
                    a3 = a[:].rearrange("p (h t) -> p h t", h=2)
                    r3 = r[:].rearrange("p (h t) -> p h t", h=2)
                    c = BU[li] * 4 + u * 4
                    pool.wait_ge(s_max, BM[li] + (u + 1) * NMX[li])
                    wait(pool, s_mt, BU[li] + u - 1)
                    pool.nop(nofuse=True)
                    nc.gpsimd.tensor_copy(m[:, :, 0, :], a3).then_inc(s_split, 1)
                    pool.wait_ge(s_split, c + 1)
                    nc.gpsimd.tensor_tensor(r3, a3, m[:, :, 0, :], ALU.subtract).then_inc(s_split, 1)
                    pool.wait_ge(s_split, c + 2)
                    pool.nop(nofuse=True)
                    nc.gpsimd.tensor_copy(m[:, :, 1, :], r3).then_inc(s_split, 1)
                    pool.wait_ge(s_split, c + 3)
                    nc.gpsimd.tensor_tensor(m[:, :, 2, :], r3, m[:, :, 1, :], ALU.subtract).then_inc(s_split, 1)
            run(pool, do)

            pool.wait_ge(s_pos, 2)
            pool.wait_ge(s_zeroed, 16 * (SLOTS // 8))
            for g in range(G):
                pool.indirect_dma_start(out=XS, out_offset=bass.IndirectOffsetOnAxis(ap=POS[:, g:g + 1], axis=0),
                                        in_=HN2[:, g, :], in_offset=None).then_inc(s_scat, 16)
            for i in range(ROUND):
                nc.gpsimd.tensor_copy(ID1[i][:], SPARE[:, i:i + 1]).then_inc(s_id, 1)
            pool.wait_ge(s_id, ROUND)
            for i in range(ROUND):
                pool.indirect_dma_start(out=YS, out_offset=bass.IndirectOffsetOnAxis(ap=ID1[i][:], axis=0),
                                        in_=TRI[:], in_offset=None).then_inc(s_back[i], 16)
            pool.wait_ge(s_ids, 1)
            with pool.Fori(0, SLOTS // ROUND) as r:
                for i in range(ROUND):
                    n = r * ROUND + i
                    pool.wait_ge(s_back[i], r * 16 + 16)
                    pool.nop(nofuse=True)
                    nc.gpsimd.tensor_copy(ID1[i][:], IDS[:, bass.ds(n, 1)]).then_inc(s_id, 1)
                    pool.wait_ge(s_id, n + ROUND + 1)
                    pool.wait_ge(s_ye, n + ROUND + 1)
                    pool.nop(nofuse=True)
                    pool.indirect_dma_start(out=YS, out_offset=bass.IndirectOffsetOnAxis(ap=ID1[i][:], axis=0),
                                            in_=YT[i], in_offset=None).then_inc(s_back[i], 16)

        @block.scalar
        def _(act):
            act.wait_ge(s_wt, 3)
            nc.scalar.mul(WQKV[:, 0:HS], PX[:, 0:HS], SCALE).then_inc(s_wready, 1)
            nc.scalar.copy(WQKV[:, HS:3 * HS], PX[:, HS:3 * HS]).then_inc(s_wready, 1)
            act.wait_ge(s_b, 16 * 6)
            for i in range(2):
                nc.scalar.mul(BIAS[:, i, 0:HS], BIAS[:, i, 0:HS], SCALE).then_inc(s_bscaled, 1)

            def parts(li, b, half, k):
                q, t0 = 2 * b + half, 4 * half
                if k == 0:
                    act.wait_ge(s_proje, 2 * (G * li + 4 * q + 4))
                else:
                    act.wait_ge(s_rem[b], 4 * li + 2 * half + 2)
                for w in range(2):
                    nc.scalar.copy(part(w, t0, b, (HI, MID)[k // 2][w]), rest(q, w)).then_inc(s_part, 1)

            def transposed(n, q):
                act.wait_ge(s_xt, n + 1)
                nc.scalar.copy(XT[:, q * 512:(q + 1) * 512], (PE[n] if n < 2 else PX)[:]).then_inc(s_xte, 1)

            for q in range(2):
                transposed(q, q)
            for k in (0, 2):
                for q in range(2):
                    parts(0, 0, q, k)
            act.wait_ge(s_small, 16 * 12)
            nc.scalar.mul(WF[:, 0:HS], WF[:, 0:HS], SCALE).then_inc(s_wready, 1)

            def do(kind, li, u0, u, k):
                L = LAYERS[li] if li < 2 else None
                if kind == "XT":
                    transposed(4 * li + 2 * u + k, 2 * u + k)
                if kind in ("CT", "NT"):
                    transposed(post_count(kind, u, k) - 1, 2 * u + k)
                if kind == "K":
                    if li == 0 and isinstance(u, int) and u == 0:
                        act.wait_ge(s_ktz, UB)
                    kt_free(act, li, u)
                    act.wait_ge(s_trans, 2 * BU[li] + 2 * u + 1)
                    nc.scalar.copy(KT[u0 % UB][0:SLOT, 0, :], PXB[0:SLOT, :]).then_inc(s_qk, 1)
                if kind == "PART" and k[1] in (0, 2):
                    parts(li, u, *k)
                if kind == "Q":
                    act.wait_ge(s_trans, 2 * BU[li] + 2 * u + 2)
                    nc.scalar.copy(QT[u0 % UB][:], PXB).then_inc(s_qk, 1)
                if kind == "EXP":
                    n = L.exp_tiles[k]["n"]
                    count = BX[li] + u * NX[li] + k
                    act.wait_ge(s_sc, count + 1)
                    e = k - L.ring
                    du = 0
                    while e < 0:
                        e += NX[li]
                        du -= 1
                    g = [i for i, gr in enumerate(L.av_groups) if gr["last"] >= e][0]
                    if li == 1 and isinstance(u, int) and u + du < 0:
                        act.wait_ge(s_av, BA[1] - NAV[0] + [i for i, gr in enumerate(LAYERS[0].av_groups)
                                                            if gr["last"] >= k][0] + 1)
                    elif not isinstance(u, int) or u + du >= 0:
                        act.wait_ge(s_av, BA[li] + (u + du) * NAV[li] + g + 1)
                    nc.scalar.activation(PR[:, k % L.ring, 0:n], exp_bank(li, u0, u, k)[:, 0:n],
                                         ACT.Exp).then_inc(s_exp, 1)
            act.wait_ge(s_zeroed, 16 * (SLOTS // 8))
            run(act, do)

            act.wait_ge(s_wt, 4)
            nc.scalar.copy(WA[:, :, B1_AT:WEXP], PM[0][:, 0:E * FC].rearrange("p (e c) -> p e c", e=E)).then_inc(s_wready, 1)
            act.wait_ge(s_pos, 3)
            act.wait_ge(s_wready, 4)
            act.wait_ge(s_we, 16 * (2 + FC))
            with act.Fori(0, SLOTS // ROUND) as r:
                for i in range(ROUND):
                    n = r * ROUND + i
                    e = act.value_load(EJ[0:1, bass.ds(n, 1)], min_val=0, max_val=E - 1)
                    act.wait_ge(s_ye, n + 1)
                    act.nop(nofuse=True)
                    nc.scalar.copy(WC[i].unsqueeze(1), WA[:, bass.ds(e, 1), :]).then_inc(s_wc, 1)
            for b in range(B):
                act.wait_ge(s_stat, b + 1)
                for g in range(b * TT, (b + 1) * TT - (DVE_SHARE if b == B - 1 else 0)):
                    nc.scalar.activation(X1[:, g, :], X[:, g, :], ACT.Identity, bias=NMR[:, g:g + 1],
                                         scale=RD[:, g:g + 1]).then_inc(s_fin, 1)

        @block.vector
        def _(dve):
            chain = [0]

            def link(ins):
                chain[0] += 1
                ins.then_inc(s_dve, 1)
                dve.wait_ge(s_dve, chain[0])

            def step(ins):
                chain[0] += 1
                ins.then_inc(s_dve, 1)

            nc.vector.memset(ZERO, 0.0).then_inc(s_zero, 1)
            for w in range(2):
                for t in range(TT):
                    nc.vector.memset(QK[:, w, t, :, :, MROW:SLOT], 0.0).then_inc(s_const, 1)
            dve.wait_ge(s_const, 2 * TT)
            for t in range(TT):
                nc.vector.memset(QK[:, 1, t, :, :, MROW:MROW + 3], 1.0).then_inc(s_const, 1)
            for e in range(E):
                nc.vector.memset(RANK[:, e:e + 1], float(E - e)).then_inc(s_const, 1)
            dve.wait_ge(s_const, NCONST)

            def projected(li, g, ps):
                bias = BIAS[:, li, :]
                b, t = divmod(g, TT)
                dve.wait_ge(s_proj, G * li + g + 1)
                if g % TT == 0 and li == 1:
                    dve.wait_ge(s_v, 3 * PAIRS * (b + 1))
                nc.vector.tensor_tensor(QKV[:, g, :], ps[:, 0:2 * HS], bias[:, 0:2 * HS], ALU.add).then_inc(s_proje, 1)
                nc.vector.tensor_tensor(VST[:, t, b, :], ps[:, 2 * HS:3 * HS], bias[:, 2 * HS:3 * HS],
                                        ALU.add).then_inc(s_proje, 1)

            def last_parts(li, b, half, w):
                q, t0 = 2 * b + half, 4 * half
                dve.wait_ge(s_rem[b], 4 * li + 2 * half + 2)
                dve.wait_ge(s_part, part_count(li, b, (half, 2)))
                nc.vector.tensor_tensor(part(w, t0, b, LO[w]), rest(q, w), part(w, t0, b, MID[w]),
                                        ALU.subtract).then_inc(s_parts[b], 1)
                for to, of in [a[1:] for a in AGAIN if a[0] == w]:
                    nc.vector.tensor_copy(part(w, t0, b, to), part(w, t0, b, of)).then_inc(s_parts[b], 1)

            def root_guess(v, y, t):
                link(nc.vector.tensor_scalar(t.bitcast(I32), v.bitcast(I32), 1, None, ALU.logical_shift_right))
                return nc.vector.tensor_scalar(y.bitcast(I32), t.bitcast(I32), -1.0, float(0x5f3759df), ALU.mult, ALU.add)

            dve.wait_ge(s_bscaled, 2)
            for g in range(TT):
                projected(0, g, PMR[g % 4])
            for q in range(2):
                dve.wait_ge(s_proje, 2 * (4 * q + 4))
                dve.wait_ge(s_part, part_count(0, 0, (q, 0)))
                for w in range(2):
                    nc.vector.tensor_tensor(rest(q, w), rest(q, w), part(w, 4 * q, 0, HI[w]),
                                            ALU.subtract).then_inc(s_rem[0], 1)
            for q in range(2):
                for w in range(2):
                    last_parts(0, 0, q, w)

            def do(kind, li, u0, u, k):
                L = LAYERS[li] if li < 2 else None
                if kind == "SUM":
                    src, n = (X, X1)[k[0]], 2 * u + k[0]
                    if li == 1 and k[0] == 0:
                        dve.wait_ge(s_res, u + 1)
                    if li == 2:
                        n = 4 + u
                        dve.wait_ge(s_woe, 4 * (u + 1))
                    wait(dve, s_norm, TT * n if k[0] == 0 else TT * n - TT + 2 * k[1] + 2)
                    tiles = (2 * k[1], 2 * k[1] + 1)
                    for t in tiles:
                        step(nc.vector.bn_stats(ST[:, t, :], src[:, u * TT + t, :]))
                    dve.wait_ge(s_dve, chain[0])
                    for t in tiles:
                        step(nc.vector.bn_aggr(MV[:, t, :], ST[:, t, :]))
                    if tiles[1] == TT - 1:
                        dve.wait_ge(s_dve, chain[0])
                        link(nc.vector.tensor_scalar(VE[:, 0:TT], MV[:, 0:TT, 1], EPS, None, ALU.add))
                        root_guess(VE[:, 0:TT], RD[:, 0:TT], SD[:, 0:TT]).then_inc(s_var, 1)
                if kind == "SCALE":
                    n, src, dst = 2 * u + k[0], (X, X1)[k[0]], (X1, X)[k[0]]
                    if li == 2:
                        n, dst = 4 + u, HN2[:, :, 0:HS]
                    if (li, u) != (2, 1):
                        dve.wait_ge(s_newton, 4 * ROOT_STEPS * (n + 1))
                    elif k[1] == 0:
                        dve.wait_ge(s_var, n + 1)
                        root_steps(dve, nc.vector, s_dve, chain[0], VE[:, 0:TT], RD[:, 0:TT], SD[:, 0:TT])
                        chain[0] += 4 * ROOT_STEPS
                    for t in (2 * k[1], 2 * k[1] + 1):
                        g = u * TT + t
                        nc.vector.tensor_scalar(dst[:, g, :], src[:, g, :], MV[:, t, 0:1], RD[:, t:t + 1],
                                                ALU.subtract, ALU.mult).then_inc(s_norm, 1)
                if kind == "AFFINE" and (li, u) == (2, 1):
                    dve.wait_ge(s_norm, TT * (4 + u) + 4 * k + 4)
                    xb = HN2[:, TT + 4 * k:TT + 4 * k + 4, 0:HS]
                    link(nc.vector.tensor_tensor(xb, xb, ROWS[:, 2:3, :].broadcast_to([P, 4, HS]), ALU.mult))
                    nc.vector.tensor_tensor(xb, xb, ROWS[:, 3:4, :].broadcast_to([P, 4, HS]), ALU.add).then_inc(s_src, 1)
                if kind == "WO":
                    g0, n = u * TT + 4 * k, 2 * (2 * u + k)
                    dve.wait_ge(s_wo, 2 * u + k + 1)
                    nc.vector.tensor_tensor(X[:, g0:g0 + 4, :], PX[:].rearrange("p (t c) -> p t c", t=4),
                                            X1[:, g0:g0 + 4, :], ALU.add).then_inc(s_woe, 1)
                    dve.wait_ge(s_woe, n + 1)
                    nc.vector.tensor_tensor(X[:, g0:g0 + 4, :], X[:, g0:g0 + 4, :],
                                            ROWS[:, 4:5, :].broadcast_to([P, 4, HS]), ALU.add).then_inc(s_woe, 1)
                if kind == "GATE":
                    dve.wait_ge(s_gate, u + 1)
                    nc.vector.tensor_tensor(LG[:, u * TT:(u + 1) * TT, :],
                                            PX[:, 0:TT * E].rearrange("p (g e) -> p g e", e=E),
                                            GB[:].unsqueeze(1).broadcast_to([P, TT, E]), ALU.add).then_inc(s_lg, 1)
                if kind == "PJ":
                    projected(li, u * TT + k, PX)
                if kind == "LO":
                    last_parts(li, u, *k)
                if kind == "K":
                    if li == 0 and isinstance(u, int) and u == 0:
                        dve.wait_ge(s_ktz, UB)
                    kt_free(dve, li, u)
                    dve.wait_ge(s_trans, 2 * BU[li] + 2 * u + 1)
                    nc.vector.tensor_copy(KT[u0 % UB][SLOT:P, 1, :], PXB[SLOT:P, :]).then_inc(s_k1, 1)
                if kind == "MAX":
                    st = L.max_steps[k]
                    pm = PM[(u0 * NMX[li] + k) % 2]
                    dve.wait_ge(s_maxmm, BM[li] + u * NMX[li] + k + 1)
                    if k == 0:
                        wait(dve, s_split, 4 * (BU[li] + u - 1))
                    c, n, step_ = st["out"]
                    o = NM[u0 % 2][:, c:c + (n - 1) * step_ + 1:step_]
                    kind_, w = st["view"]
                    if kind_ == "flat":
                        i = pm[:]
                    else:
                        i = pm[:].rearrange("p (k n) -> p k n", k=2)[:, :, 0:w]
                    nc.vector.tensor_reduce(o, i, AX_X, ALU.max, negate=True).then_inc(s_max, 1)
                if kind == "MT":
                    dve.wait_ge(s_mt, BU[li] + u + 1)
                    wait(dve, s_mrow, 32 * (BU[li] + u - 1))
                    nc.vector.tensor_copy(MT[u0 % 2][:], PXB[0:6 * TT, 0:P]).then_inc(s_mte, 1)
                if kind == "OE":
                    dve.wait_ge(s_av, BA[li] + (u + 1) * NAV[li])
                    wait(dve, s_ot, BU[li] + u)
                    nc.vector.tensor_copy(OS[:], PO[:]).then_inc(s_oe, 1)
                if kind == "OT":
                    px = PX[:].rearrange("p (c h a d) -> p c h a d", c=4, h=2, a=2)
                    rs = RS[:].rearrange("p (c h a) -> p c h a", c=4, h=2)
                    dve.wait_ge(s_ot, BU[li] + u + 1)
                    wait(dve, s_ctx, 2 * (BU[li] + u))
                    nc.vector.reciprocal(RS[:], PX[:].rearrange("p (c d) -> p c d", d=32)[:, :, D]).then_inc(s_rs, 1)
                    dve.wait_ge(s_rs, BU[li] + u + 1)
                    for h in range(2):
                        o = CTX[:].rearrange("p t b c -> p t (b c)")[:, :, bass.ds((u * 2 + h) * D, D)] \
                            .rearrange("p (a c) d -> p c a d", a=2)
                        nc.vector.tensor_tensor(o, px[:, :, h, :, 0:D],
                                                rs[:, :, h, :].unsqueeze(3).broadcast_to([P, 4, 2, D]),
                                                ALU.mult).then_inc(s_ctx, 1)
            run(dve, do)

            dve.wait_ge(s_lg, 2)
            rank = RANK[:].unsqueeze(1).broadcast_to([P, G, E])
            link(nc.vector.tensor_reduce(LM[:], LG[:], AX_X, ALU.max))
            link(nc.vector.tensor_tensor(LE[:], LG[:], LM[:].unsqueeze(2).broadcast_to([P, G, E]), ALU.is_ge))
            link(nc.vector.tensor_tensor(LE[:], LE[:], rank, ALU.mult))
            link(nc.vector.tensor_reduce(LM[:], LE[:], AX_X, ALU.max))
            nc.vector.tensor_tensor(OH[:], LE[:], LM[:].unsqueeze(2).broadcast_to([P, G, E]),
                                    ALU.is_equal).then_inc(s_oh, 1)
            dve.wait_ge(s_oh, 1)
            dve.wait_ge(s_count, 3)
            dve.wait_ge(s_jc, SLOTS + 1)
            step(nc.vector.tensor_copy(PREF[:], PO[:, 0:G * E].rearrange("p (g e) -> p g e", e=E)))
            step(nc.vector.tensor_copy(TOT[:], PX[:, 0:G * E].rearrange("p (g e) -> p g e", e=E)))
            link(nc.vector.tensor_copy(CUM[0][:], PX[:, 0:G * E].rearrange("p (g e) -> p g e", e=E)))
            link(nc.vector.tensor_tensor(POSF[:], KC[:], PX[:, 2 * P:2 * P + 1].broadcast_to([P, G]), ALU.add))
            step(nc.vector.tensor_copy(SPARE[:], POSF[:, 0:ROUND]))
            nc.vector.tensor_scalar(HN2[:, :, HS], POSF[:], float(ROUND * P), None, ALU.add).then_inc(s_pos, 1)
            dve.wait_ge(s_pos, 1)
            a, b_ = CUM
            for d in (1, 2, 4, 8):
                step(nc.vector.tensor_copy(b_[:, 0:d, :], a[:, 0:d, :]))
                link(nc.vector.tensor_tensor(b_[:, d:, :], a[:, d:, :], a[:, :G - d, :], ALU.add))
                a, b_ = b_, a
            cmp_ = CMP[:].rearrange("p s e -> p (s e)")[:, 0:E * G].rearrange("p (e g) -> p e g", e=E)
            link(nc.vector.tensor_tensor(cmp_, a[:, G - 1, :].unsqueeze(2).broadcast_to([P, E, G]),
                                         KC[:].unsqueeze(1).broadcast_to([P, E, G]), ALU.is_gt))
            link(nc.vector.tensor_reduce(TL[:], cmp_, AX_X, ALU.add))
            link(nc.vector.tensor_copy(EN[0][:], TL[:]))
            c, d_ = EN
            for d in (1, 2, 4):
                step(nc.vector.tensor_copy(d_[:, 0:d], c[:, 0:d]))
                link(nc.vector.tensor_tensor(d_[:, d:], c[:, d:], c[:, :E - d], ALU.add))
                c, d_ = d_, c
            link(nc.vector.tensor_tensor(S128[:], c[:], TL[:], ALU.subtract))
            link(nc.vector.tensor_scalar(S128[:], S128[:], float(P), None, ALU.mult))
            link(nc.vector.tensor_tensor(PREF[:], PREF[:], a[:], ALU.add))
            link(nc.vector.tensor_tensor(PREF[:], PREF[:], TOT[:], ALU.subtract))
            link(nc.vector.tensor_tensor(PREF[:], PREF[:], S128[:].unsqueeze(1).broadcast_to([P, G, E]), ALU.add))
            link(nc.vector.tensor_tensor(PREF[:], PREF[:], OH[:], ALU.mult))
            link(nc.vector.tensor_reduce(POSF[:], PREF[:], AX_X, ALU.add))
            nc.vector.tensor_copy(POS[:], POSF[:]).then_inc(s_pos, 1)
            link(nc.vector.tensor_tensor(CMP[:], c[:].unsqueeze(1).broadcast_to([P, SLOTS, E]),
                                         JC[:].unsqueeze(2).broadcast_to([P, SLOTS, E]), ALU.is_le))
            link(nc.vector.tensor_reduce(EJF[:], CMP[:], AX_X, ALU.add))
            nc.vector.tensor_scalar(EJ[:], EJF[:], float(E - 1), None, ALU.min).then_inc(s_pos, 1)
            dve.wait_ge(s_pos, 3)
            link(nc.vector.tensor_tensor(X[:], X[:], X1[:], ALU.add))
            for q in range(SLOTS // 4):
                dve.wait_ge(s_xt, 16 + q + 1)
                nc.vector.tensor_copy(XST[:, q * 512:(q + 1) * 512], PE[q % 2][:]).then_inc(s_xte, 1)
            for i in range(SLOTS // 8):
                dve.wait_ge(s_xs[i], 16)
            nc.vector.tensor_tensor(IDS[:].rearrange("p (r i) -> p r i", i=ROUND),
                                    XSB[:, :, HS].rearrange("p (r i) -> p r i", i=ROUND),
                                    SPARE[:].unsqueeze(1).broadcast_to([P, SLOTS // ROUND, ROUND]),
                                    ALU.max).then_inc(s_ids, 1)
            dve.nop(nofuse=True).then_inc(s_hte, ROUND * FC)
            dve.nop(nofuse=True).then_inc(s_ye, ROUND)
            with dve.Fori(0, SLOTS // ROUND) as r:
                for step_, i in MOE_ORDER:
                    n = r * ROUND + i
                    if step_ == "w1":
                        dve.wait_ge(s_h, n + ROUND + 1)
                        dve.wait_ge(s_y, n + 1)
                        for f in range(FC):
                            nc.vector.tensor_scalar(HT[i][:, f * P:(f + 1) * P], TB[i][:, f * P:(f + 1) * P],
                                                    WC[i][:, B1_AT + f:B1_AT + f + 1], 0.0,
                                                    ALU.add, ALU.max).then_inc(s_hte, 1)
                    else:
                        dve.wait_ge(s_y, n + ROUND + 1)
                        dve.wait_ge(s_back[i], r * 16 + 16)
                        nc.vector.tensor_tensor(YT[i], YB[i], WC[i][:, B2_AT:B1_AT], ALU.add).then_inc(s_ye, 1)
            for b in range(B):
                g0, g1 = b * TT, (b + 1) * TT
                dve.wait_ge(s_moe[b], 16)
                link(nc.vector.tensor_tensor(X[:, g0:g1, :], X[:, g0:g1, :], MOE[:, g0:g1, :], ALU.add))
                for g in range(g0, g1):
                    step(nc.vector.bn_stats(ST[:, g, :], X[:, g, :]))
                dve.wait_ge(s_dve, chain[0])
                for g in range(g0, g1):
                    step(nc.vector.bn_aggr(MV[:, g, :], ST[:, g, :]))
                dve.wait_ge(s_dve, chain[0])
                link(nc.vector.tensor_scalar(VE[:, g0:g1], MV[:, g0:g1, 1], EPS, None, ALU.add))
                link(root_guess(VE[:, g0:g1], RD[:, g0:g1], SD[:, g0:g1]))
                root_steps(dve, nc.vector, s_dve, chain[0], VE[:, g0:g1], RD[:, g0:g1], SD[:, g0:g1])
                chain[0] += 4 * ROOT_STEPS
                link(nc.vector.tensor_tensor(NMR[:, g0:g1], MV[:, g0:g1, 0], RD[:, g0:g1], ALU.mult))
                nc.vector.tensor_scalar(NMR[:, g0:g1], NMR[:, g0:g1], -1.0, None, ALU.mult).then_inc(s_stat, 1)
                if b == B - 1:
                    for g in range(g1 - DVE_SHARE, g1):
                        nc.vector.tensor_scalar(X1[:, g, :], X[:, g, :], MV[:, g, 0:1], RD[:, g:g + 1],
                                                ALU.subtract, ALU.mult).then_inc(s_fin1, 1)

        @block.tensor
        def _(pe):
            pe.wait_ge(s_ident, 2)
            pe.wait_ge(s_w, 16 * 3)
            for i in range(3):
                pe.transpose(PX[:, i * P:(i + 1) * P], WRAW[:, i, :], IDF[:]).then_inc(s_wt, 1)

            def tile_transposes(q, src, bank):
                for t in range(4):
                    ins = pe.transpose(bank[:, t * P:(t + 1) * P], src(4 * (q % 4) + t), IDF[:])
                ins.then_inc(s_xt, 1)

            def projection(li, g, bank):
                pe.wait_ge(s_xte, 4 * li + g // 4 + 1)
                pe.matmul(bank[:, 0:3 * HS], XT[:, g * P:(g + 1) * P], (WQKV, WF)[li][:], start=True,
                          stop=True).then_inc(s_proj, 1)

            pe.wait_ge(s_x[0], 16 * 5)
            for q in range(2):
                tile_transposes(q, lambda g: X[:, g, :], PE[q])
            pe.wait_ge(s_wready, 2)
            for g in range(TT):
                if g >= 4:
                    pe.wait_ge(s_proje, 2 * (g - 3))
                projection(0, g, PMR[g % 4])

            def shared_free(kind, li, u0, u, k):
                if SHARED[kind, li, u0, k] is None:
                    return
                k2, l2, u2, x2 = SHARED[kind, li, u0, k]
                if k2 == "XT":
                    pe.wait_ge(s_xte, 4 * l2 + 2 * u2 + x2 + 1)
                    return
                if k2 in ("CT", "NT"):
                    pe.wait_ge(s_xte, post_count(k2, u2, x2))
                    return
                if k2 == "WO":
                    pe.wait_ge(s_woe, 2 * (2 * u2 + x2) + 1)
                    return
                if k2 == "GATE":
                    pe.wait_ge(s_lg, u2 + 1)
                    return
                if k2 == "PJ":
                    pe.wait_ge(s_proje, 2 * (G * l2 + TT * u2 + x2 + 1))
                    return
                v = u + (u2 - u0) if kind in ("K", "Q", "MT", "OT") and l2 == li else u2
                if k2 == "K":
                    pe.wait_ge(s_k1, BU[l2] + v + 1)
                s, value = {"K": (s_qk, 2 * (BU[l2] + v) + 1), "Q": (s_qk, 2 * (BU[l2] + v) + 2),
                            "MT": (s_mte, BU[l2] + v + 1), "OT": (s_ctx, 2 * (BU[l2] + v + 1))}[k2]
                pe.wait_ge(s, value)

            def do(kind, li, u0, u, k):
                L = LAYERS[li] if li < 2 else None
                q, kt, vb = QT[u0 % UB], KT[u0 % UB], VB[u0 % 2]
                if kind == "XT":
                    if li == 0:
                        pe.wait_ge(s_x[1], 16 * 5)
                    else:
                        pe.wait_ge(s_src, 2 * u + k + 1)
                    shared_free(kind, li, u0, u, k)
                    tile_transposes(4 * li + 2 * u + k, lambda g: X[:, g, :], PX)
                if kind == "PJ":
                    if li == 1:
                        pe.wait_ge(s_wready, 3)
                        pe.wait_ge(s_small, 16 * 12)
                    shared_free(kind, li, u0, u, k)
                    projection(li, u * TT + k, PX)
                if kind == "CT":
                    pe.wait_ge(s_ctx, 2 * (UNITS + PAIRS * (u + 1)))
                    shared_free(kind, li, u0, u, k)
                    tile_transposes(2 * u + k, lambda g: CTX[:, g % TT, g // TT, :], PX)
                if kind == "WO":
                    if u == 0:
                        pe.wait_ge(s_small, 16 * 12)
                    pe.wait_ge(s_xte, post_count("CT", u, k))
                    shared_free(kind, li, u0, u, k)
                    for t in range(4):
                        g = u * TT + 4 * k + t
                        ins = pe.matmul(PX[:, t * P:(t + 1) * P], XT[:, g * P:(g + 1) * P], WO[:], start=True, stop=True)
                    ins.then_inc(s_wo, 1)
                if kind == "NT":
                    pe.wait_ge(s_src, 4 + 2 * u + k + 1)
                    shared_free(kind, li, u0, u, k)
                    tile_transposes(2 * u + k, lambda g: HN2[:, g, 0:HS], PX)
                if kind == "GATE":
                    pe.wait_ge(s_xte, post_count("NT", u, 1))
                    shared_free(kind, li, u0, u, k)
                    for t in range(TT):
                        g = u * TT + t
                        ins = pe.matmul(PX[:, t * E:(t + 1) * E], XT[:, g * P:(g + 1) * P], GW[:], start=True, stop=True)
                    ins.then_inc(s_gate, 1)
                if kind in ("K", "Q"):
                    w = 1 if kind == "K" else 0
                    shared_free(kind, li, u0, u, k)
                    pe.wait_ge(s_parts[0], 16 * (li + 1))
                    if u0 >= L.late["K"]:
                        pe.wait_ge(s_parts[1], 16 * (li + 1))
                    if u0 == 0:
                        pe.wait_ge(s_ktz, UB)
                        pe.wait_ge(s_const, NCONST)
                    for t in range(TT):
                        src = QK[:, w, t, :, :, :].rearrange("p b h s -> p (b h s)")[:, bass.ds(u * P, P)]
                        ins = pe.transpose(PXB[:, t * P:(t + 1) * P], src, IDB[:])
                    ins.then_inc(s_trans, 1)
                if kind == "MAX":
                    st = L.max_steps[k]
                    pm = PM[(u0 * NMX[li] + k) % 2]
                    if k == 0:
                        pe.wait_ge(s_qk, 2 * (BU[li] + u + 1))
                        pe.wait_ge(s_k1, BU[li] + u + 1)
                    count = BM[li] + u * NMX[li] + k
                    wait(pe, s_max, count - 1)
                    for item in st["mms"]:
                        h, m = item if isinstance(item, tuple) else (st["h"], item)
                        (r0, r1), (l0, ln), (c0, cn) = m["rows"], m["left"], m["right"]
                        o = m["bank"] * 512 + m["col"]
                        ins = pe.matmul(pm[r0:r1, o:o + cn], q[:, l0:l0 + ln], kt[:, h, c0:c0 + cn],
                                        start=True, stop=True)
                    ins.then_inc(s_maxmm, 1)
                if kind == "EXP":
                    count = BX[li] + u * NX[li] + k
                    if k == 0:
                        pe.wait_ge(s_mrow, 32 * (BU[li] + u + 1))
                    if not (li == 1 and isinstance(u, int) and u == UNITS - 1) or k < 2:
                        wait(pe, s_exp, count - 1)
                    elif k < 6:
                        pe.wait_ge(s_max, BM[1] + UNITS * NMX[1])
                    else:
                        pe.wait_ge(s_exp, count - 5)
                    ps = exp_bank(li, u0, u, k)
                    for h, m in L.exp_tiles[k]["mms"]:
                        (r0, r1), (l0, ln), (c0, cn) = m["rows"], m["left"], m["right"]
                        ins = pe.matmul(ps[r0:r1, m["col"]:m["col"] + cn], kt[:, h, l0:l0 + ln], q[:, c0:c0 + cn],
                                        start=True, stop=True)
                    ins.then_inc(s_sc, 1)
                if kind == "AV":
                    gr = L.av_groups[k]
                    pe.wait_ge(s_exp, BX[li] + u * NX[li] + gr["last"] + 1)
                    if k == 0:
                        pe.wait_ge(s_v, (3 * UNITS if li else 0) + len(L.kinds) * (u + 1))
                        wait(pe, s_oe, BU[li] + u)
                    for h, half, e, (c0, cn), kd, t, o, first, last in gr["mms"]:
                        r = 64 * h + 32 * half
                        ins = pe.matmul(PO[r:r + 32, o:o + cn], vb[:, L.kinds.index(kd), t, h, :],
                                        PR[:, e % L.ring, c0:c0 + cn], start=first, stop=last,
                                        skip_group_check=True, tile_position=(0, r))
                    ins.then_inc(s_av, 1)
                if kind == "MT":
                    shared_free(kind, li, u0, u, k)
                    pe.wait_ge(s_split, 4 * (BU[li] + u + 1))
                    pe.nop(nofuse=True)
                    pe.transpose(PXB[0:6 * TT, 0:P], MS[u0 % 2][:].rearrange("p h s t -> p (h s t)"),
                                 IDB[:]).then_inc(s_mt, 1)
                if kind == "OT":
                    shared_free(kind, li, u0, u, k)
                    pe.wait_ge(s_oe, BU[li] + u + 1)
                    for c in range(4):
                        ins = pe.transpose(PX[:, c * P:(c + 1) * P], OS[:, c * P:(c + 1) * P], IDF[:])
                    ins.then_inc(s_ot, 1)

            run(pe, do)

            pe.wait_ge(s_max, BM[1] + UNITS * NMX[1])
            pe.transpose(PM[0][:, 0:E * FC], B1R[:], IDF[0:E * FC, 0:E * FC]).then_inc(s_wt, 1)
            pe.wait_ge(s_oe, 2 * UNITS)
            pe.wait_ge(s_lg, 2)
            pe.wait_ge(s_oh, 1)
            pe.wait_ge(s_tri, 3)
            oh = OH[:].rearrange("p g e -> p (g e)")
            pe.matmul(PO[:, 0:G * E], TRI[:], oh, start=True, stop=True).then_inc(s_count, 1)
            pe.matmul(PX[:, 0:G * E], ONES[:], oh, start=True, stop=True).then_inc(s_count, 1)
            pe.matmul(PX[:, 2 * P:2 * P + 1], TRI[:], ONES[:, 0:1], start=True, stop=True).then_inc(s_count, 1)
            for q in range(SLOTS // 4):
                pe.wait_ge(s_xs[q // 2], 16)
                pe.wait_ge(s_xte, 16 + q - 1)
                for t in range(4):
                    ins = pe.transpose(PE[q % 2][:, t * P:(t + 1) * P], XSB[:, 4 * q + t, 0:HS], IDF[:])
                ins.then_inc(s_xt, 1)
            pe.wait_ge(s_xte, 16 + SLOTS // 4)
            pe.wait_ge(s_pos, 3)
            pe.nop(nofuse=True).then_inc(s_y, ROUND)
            pe.nop(nofuse=True).then_inc(s_h, ROUND)
            with pe.Fori(0, SLOTS // ROUND) as r:
                for step_, i in MOE_ORDER:
                    n = r * ROUND + i
                    if step_ == "w1":
                        pe.wait_ge(s_wc, n + 1)
                        pe.wait_ge(s_hte, (n + 1) * FC)
                        for f in range(FC):
                            ins = pe.matmul(TB[i][:, f * P:(f + 1) * P], WC[i][:, f * P:(f + 1) * P],
                                            XST[:, bass.ds(n * P, P)], start=True, stop=True)
                        ins.then_inc(s_h, 1)
                    else:
                        pe.wait_ge(s_hte, (n + ROUND + 1) * FC)
                        pe.wait_ge(s_ye, n + 1)
                        for f in range(FC):
                            ins = pe.matmul(YB[i], HT[i][:, f * P:(f + 1) * P],
                                            WC[i][:, W2_AT + f * HS:W2_AT + (f + 1) * HS],
                                            start=(f == 0), stop=(f == FC - 1))
                        ins.then_inc(s_y, 1)


_INS = ['hidden_states', 'Wq', 'bq', 'Wk', 'bk', 'Wv', 'bv']
_FFN = ['ln1_g', 'ln1_b', 'ln2_g', 'ln2_b', 'wq', 'bq', 'wk', 'bk', 'wv', 'bv', 'wo', 'bo', 'gate_w', 'gate_b',
        'w1', 'b1', 'w2', 'b2']
_NAMES = ['L0_attn_' + n for n in _INS] + ['L0_ffn_' + n for n in _FFN]


def kernel(**inputs):
    import numpy as _np
    import concourse.bacc as _bacc
    from concourse import mybir as _mybir
    from concourse.bass_utils import run_bass_kernel_spmd as _run

    nc = _bacc.Bacc("TRN2", target_bir_lowering=False, num_devices=1)
    arrays, args = {}, []
    for name in _NAMES:
        a = _np.ascontiguousarray(inputs[name])
        arrays[f"in_{name}_dram"] = a
        args.append(nc.dram_tensor(f"in_{name}_dram", a.shape, _mybir.dt.from_np(a.dtype), kind="ExternalInput").ap())
    args.append(nc.dram_tensor("out_0_dram", (B, SEQ, HS), F32, kind="ExternalOutput").ap())
    build(nc, *args)
    r = _run(nc, [arrays], core_ids=[0])
    return r.results[0]["out_0_dram"]
```
